# Optimizing a Trainium2 kernel written in Bass

```python
import numpy as np
import jax
import jax.numpy as jnp

def _softmax(x, axis=-1):
    return jax.nn.softmax(x, axis=axis)

def _gelu(x):
    return jax.nn.gelu(x, approximate=True)

def _silu(x):
    return jax.nn.silu(x)

def _sigmoid(x):
    return jax.nn.sigmoid(x)

def _layernorm(x, axis=-1, eps=1e-05):
    m = jnp.mean(x, axis=axis, keepdims=True)
    v = jnp.var(x, axis=axis, keepdims=True)
    return (x - m) / jnp.sqrt(v + eps)

def _scatter_add(tgt, idx, src, axis=0):
    return tgt.at[idx].add(src)

def _segment_sum(src, seg, n):
    return jax.ops.segment_sum(src, seg, n)
kernel_name = 'mk_seq_postln_d1_jaxref_r8_398a40'

def setup_inputs(seed: int=0):
    np.random.seed(seed)
    _w = jnp.asarray

    def _L0_attn_setup():
        import jax, jax.numpy as jnp
        import numpy as np
        D_MODEL = 128
        N_HEADS = 16
        LATENT_HEADS = 8
        LATENT_DIM = 64
        N_LATENTS = 64
        WINDOW = 32
        HEAD_DIM = D_MODEL // N_HEADS
        LAT_HD = LATENT_DIM // LATENT_HEADS
        B, S = (2, 512)

        def _pool_to_latents(x):
            Bx, Sx, C = x.shape
            chunk = max(1, Sx // N_LATENTS)
            return x.reshape(Bx, N_LATENTS, chunk, C).mean(axis=2)

        def _local_window_attn(Q, K, V):
            Bx, H, Sx, D = Q.shape
            W = WINDOW
            nb = Sx // W
            Qb = Q.reshape(Bx, H, nb, W, D)
            Kp = jnp.pad(K, ((0, 0), (0, 0), (W, 0), (0, 0))).reshape(Bx, H, nb + 1, W, D)
            Vp = jnp.pad(V, ((0, 0), (0, 0), (W, 0), (0, 0))).reshape(Bx, H, nb + 1, W, D)
            Kw = jnp.concatenate([Kp[:, :, :-1], Kp[:, :, 1:]], axis=3)
            Vw = jnp.concatenate([Vp[:, :, :-1], Vp[:, :, 1:]], axis=3)
            i = jnp.arange(W)[:, None]
            j = jnp.arange(2 * W)[None, :]
            base = (j > i) & (j <= i + W)
            blk0 = (jnp.arange(nb) > 0)[:, None, None] | (j >= W)[None, :, :]
            mask = base[None, :, :] & blk0
            sc = jnp.einsum('bhnid,bhnjd->bhnij', Qb, Kw) / np.sqrt(D).astype(np.float32)
            sc = jnp.where(mask[None, None], sc, -jnp.inf)
            p = jax.nn.softmax(sc, axis=-1)
            out = jnp.einsum('bhnij,bhnjd->bhnid', p, Vw)
            return out.reshape(Bx, H, Sx, D)
        key = jax.random.key(seed)
        ks = jax.random.split(key, 11)
        std = 0.02
        w = lambda k, shp: jax.random.normal(k, shp, jnp.float32) * std
        return {'x': jax.random.normal(ks[0], (B, S, D_MODEL), jnp.float32), 'wq': w(ks[1], (D_MODEL, D_MODEL)), 'wk': w(ks[2], (D_MODEL, D_MODEL)), 'wv': w(ks[3], (D_MODEL, D_MODEL)), 'wgq': w(ks[4], (D_MODEL, LATENT_DIM)), 'wgk': w(ks[5], (D_MODEL, LATENT_DIM)), 'wgv': w(ks[6], (D_MODEL, LATENT_DIM)), 'r_out_w': w(ks[7], (LATENT_DIM, D_MODEL)), 'gate_local_w': w(ks[8], (N_HEADS, HEAD_DIM)), 'gate_remote_w': w(ks[9], (N_HEADS, HEAD_DIM)), 'w_out': w(ks[10], (D_MODEL, D_MODEL))}
    _L0_attn_in = _L0_attn_setup()

    def _L0_ffn_setup():
        import jax, jax.numpy as jnp
        import numpy as np
        D_IN, D_HID = (128, 512)

        def _ternary(key, shape):
            return jax.random.randint(key, shape, -1, 2).astype(jnp.float32)

        def _tlin(x, w, s):
            return jnp.einsum('bsi,oi->bso', x, w) * s
        key = jax.random.key(seed)
        ks = jax.random.split(key, 12)
        inv = lambda fan: 1.0 / np.sqrt(fan).astype(np.float32)
        return {'x': jax.random.normal(ks[0], (4, 256, D_IN), dtype=jnp.float32), 'w1_w': _ternary(ks[1], (D_HID, D_IN)), 'w1_s': jax.random.uniform(ks[2], (D_HID,), dtype=jnp.float32) * inv(D_IN), 'w2_w': _ternary(ks[3], (D_HID, D_IN)), 'w2_s': jax.random.uniform(ks[4], (D_HID,), dtype=jnp.float32) * inv(D_IN), 'h1_w': _ternary(ks[5], (D_HID, D_HID)), 'h1_s': jax.random.uniform(ks[6], (D_HID,), dtype=jnp.float32) * inv(D_HID), 'h2_w': _ternary(ks[7], (D_HID, D_HID)), 'h2_s': jax.random.uniform(ks[8], (D_HID,), dtype=jnp.float32) * inv(D_HID), 'w3_w': _ternary(ks[9], (D_IN, D_HID)), 'w3_s': jax.random.uniform(ks[10], (D_IN,), dtype=jnp.float32) * inv(D_HID)}
    _L0_ffn_in = _L0_ffn_setup()
    _d = {'L0_attn_x': _L0_attn_in['x'], 'L0_attn_wq': _L0_attn_in['wq'], 'L0_attn_wk': _L0_attn_in['wk'], 'L0_attn_wv': _L0_attn_in['wv'], 'L0_attn_wgq': _L0_attn_in['wgq'], 'L0_attn_wgk': _L0_attn_in['wgk'], 'L0_attn_wgv': _L0_attn_in['wgv'], 'L0_attn_r_out_w': _L0_attn_in['r_out_w'], 'L0_attn_gate_local_w': _L0_attn_in['gate_local_w'], 'L0_attn_gate_remote_w': _L0_attn_in['gate_remote_w'], 'L0_attn_w_out': _L0_attn_in['w_out'], 'L0_ffn_w1_w': _L0_ffn_in['w1_w'], 'L0_ffn_w1_s': _L0_ffn_in['w1_s'], 'L0_ffn_w2_w': _L0_ffn_in['w2_w'], 'L0_ffn_w2_s': _L0_ffn_in['w2_s'], 'L0_ffn_h1_w': _L0_ffn_in['h1_w'], 'L0_ffn_h1_s': _L0_ffn_in['h1_s'], 'L0_ffn_h2_w': _L0_ffn_in['h2_w'], 'L0_ffn_h2_s': _L0_ffn_in['h2_s'], 'L0_ffn_w3_w': _L0_ffn_in['w3_w'], 'L0_ffn_w3_s': _L0_ffn_in['w3_s']}
    _x0 = _d['L0_attn_x']
    _d['L0_attn_x'] = jax.random.normal(jax.random.fold_in(jax.random.key(seed), 1), (2, 1024, 128), dtype=_x0.dtype)
    del _x0
    return _d

def reference(L0_attn_x, L0_attn_wq, L0_attn_wk, L0_attn_wv, L0_attn_wgq, L0_attn_wgk, L0_attn_wgv, L0_attn_r_out_w, L0_attn_gate_local_w, L0_attn_gate_remote_w, L0_attn_w_out, L0_ffn_w1_w, L0_ffn_w1_s, L0_ffn_w2_w, L0_ffn_w2_s, L0_ffn_h1_w, L0_ffn_h1_s, L0_ffn_h2_w, L0_ffn_h2_s, L0_ffn_w3_w, L0_ffn_w3_s):

    def _L0_attn_ref(x, wq, wk, wv, wgq, wgk, wgv, r_out_w, gate_local_w, gate_remote_w, w_out):
        import jax, jax.numpy as jnp
        import numpy as np
        D_MODEL = 128
        N_HEADS = 16
        LATENT_HEADS = 8
        LATENT_DIM = 64
        N_LATENTS = 64
        WINDOW = 32
        HEAD_DIM = D_MODEL // N_HEADS
        LAT_HD = LATENT_DIM // LATENT_HEADS
        B, S = (2, 512)

        def _pool_to_latents(x):
            Bx, Sx, C = x.shape
            chunk = max(1, Sx // N_LATENTS)
            return x.reshape(Bx, N_LATENTS, chunk, C).mean(axis=2)

        def _local_window_attn(Q, K, V):
            Bx, H, Sx, D = Q.shape
            W = WINDOW
            nb = Sx // W
            Qb = Q.reshape(Bx, H, nb, W, D)
            Kp = jnp.pad(K, ((0, 0), (0, 0), (W, 0), (0, 0))).reshape(Bx, H, nb + 1, W, D)
            Vp = jnp.pad(V, ((0, 0), (0, 0), (W, 0), (0, 0))).reshape(Bx, H, nb + 1, W, D)
            Kw = jnp.concatenate([Kp[:, :, :-1], Kp[:, :, 1:]], axis=3)
            Vw = jnp.concatenate([Vp[:, :, :-1], Vp[:, :, 1:]], axis=3)
            i = jnp.arange(W)[:, None]
            j = jnp.arange(2 * W)[None, :]
            base = (j > i) & (j <= i + W)
            blk0 = (jnp.arange(nb) > 0)[:, None, None] | (j >= W)[None, :, :]
            mask = base[None, :, :] & blk0
            sc = jnp.einsum('bhnid,bhnjd->bhnij', Qb, Kw) / np.sqrt(D).astype(np.float32)
            sc = jnp.where(mask[None, None], sc, -jnp.inf)
            p = jax.nn.softmax(sc, axis=-1)
            out = jnp.einsum('bhnij,bhnjd->bhnid', p, Vw)
            return out.reshape(Bx, H, Sx, D)
        Bx, Sx, _ = x.shape
        chunk = max(1, Sx // N_LATENTS)
        Q = (x @ wq).reshape(Bx, Sx, N_HEADS, HEAD_DIM).transpose(0, 2, 1, 3)
        K = (x @ wk).reshape(Bx, Sx, N_HEADS, HEAD_DIM).transpose(0, 2, 1, 3)
        V = (x @ wv).reshape(Bx, Sx, N_HEADS, HEAD_DIM).transpose(0, 2, 1, 3)
        local = _local_window_attn(Q, K, V)
        GQ = (x @ wgq).reshape(Bx, Sx, LATENT_HEADS, LAT_HD).transpose(0, 2, 1, 3)
        GK = _pool_to_latents(x @ wgk).reshape(Bx, N_LATENTS, LATENT_HEADS, LAT_HD).transpose(0, 2, 1, 3)
        GV = _pool_to_latents(x @ wgv).reshape(Bx, N_LATENTS, LATENT_HEADS, LAT_HD).transpose(0, 2, 1, 3)
        lsc = jnp.einsum('bhsd,bhnd->bhsn', GQ, GK) / np.sqrt(LAT_HD).astype(np.float32)
        lmask = jnp.arange(N_LATENTS)[None, :] <= (jnp.arange(Sx) // chunk)[:, None]
        lsc = jnp.where(lmask[None, None], lsc, -jnp.inf)
        lp = jax.nn.softmax(lsc, axis=-1)
        rem = jnp.einsum('bhsn,bhnd->bhsd', lp, GV)
        rem = rem.transpose(0, 2, 1, 3).reshape(Bx, Sx, LATENT_DIM) @ r_out_w
        rem = rem.reshape(Bx, Sx, N_HEADS, HEAD_DIM).transpose(0, 2, 1, 3)
        gl = jax.nn.sigmoid(jnp.einsum('bhsd,hd->bhs', Q, gate_local_w))[..., None]
        gr = jax.nn.sigmoid(jnp.einsum('bhsd,hd->bhs', Q, gate_remote_w))[..., None]
        out = gl * local + gr * rem
        out = out.transpose(0, 2, 1, 3).reshape(Bx, Sx, D_MODEL)
        return out @ w_out

    def _L0_ffn_ref(x, w1_w, w1_s, w2_w, w2_s, h1_w, h1_s, h2_w, h2_s, w3_w, w3_s):
        import jax, jax.numpy as jnp
        import numpy as np
        D_IN, D_HID = (128, 512)

        def _ternary(key, shape):
            return jax.random.randint(key, shape, -1, 2).astype(jnp.float32)

        def _tlin(x, w, s):
            return jnp.einsum('bsi,oi->bso', x, w) * s
        h = jax.nn.silu(_tlin(x, w1_w, w1_s)) * _tlin(x, w2_w, w2_s)
        h = jax.nn.gelu(_tlin(h, h1_w, h1_s), approximate=False)
        h = jax.nn.gelu(_tlin(h, h2_w, h2_s), approximate=False)
        return _tlin(h, w3_w, w3_s)
    x = L0_attn_x
    x = _layernorm(x + _L0_attn_ref(x, L0_attn_wq, L0_attn_wk, L0_attn_wv, L0_attn_wgq, L0_attn_wgk, L0_attn_wgv, L0_attn_r_out_w, L0_attn_gate_local_w, L0_attn_gate_remote_w, L0_attn_w_out), axis=-1)
    x = _layernorm(x + _L0_ffn_ref(x, L0_ffn_w1_w, L0_ffn_w1_s, L0_ffn_w2_w, L0_ffn_w2_s, L0_ffn_h1_w, L0_ffn_h1_s, L0_ffn_h2_w, L0_ffn_h2_s, L0_ffn_w3_w, L0_ffn_w3_s), axis=-1)
    return x

_drawn_inputs = setup_inputs


def setup_inputs(seed=0):
    import zlib

    import numpy as np

    out = dict(_drawn_inputs(seed))
    spreads = {}
    factors = {'L0_attn_wq': 8.0,
     'L0_attn_wk': 8.0,
     'L0_attn_wv': 8.0,
     'L0_attn_wgq': 8.0,
     'L0_attn_wgk': 8.0,
     'L0_attn_wgv': 8.0,
     'L0_attn_r_out_w': 8.0,
     'L0_attn_gate_local_w': 8.0,
     'L0_attn_gate_remote_w': 8.0,
     'L0_attn_w_out': 8.0,
     'L0_ffn_w1_w': 8.0,
     'L0_ffn_w1_s': 8.0,
     'L0_ffn_w2_w': 8.0,
     'L0_ffn_w2_s': 8.0,
     'L0_ffn_h1_w': 8.0,
     'L0_ffn_h1_s': 8.0,
     'L0_ffn_h2_w': 8.0,
     'L0_ffn_h2_s': 8.0,
     'L0_ffn_w3_w': 8.0,
     'L0_ffn_w3_s': 8.0}
    for name, (base, spread) in spreads.items():
        noise = np.random.default_rng([zlib.crc32(name.encode()), seed]).standard_normal(out[name].shape)
        drawn = base * np.exp(spread * noise) if base else spread * noise
        out[name] = jnp.asarray(drawn.astype(out[name].dtype))
    for name, factor in factors.items():
        out[name] = (out[name] * factor).astype(out[name].dtype)
    return out
```

```python
from contextlib import ExitStack

import numpy as np

import concourse.bass as bass
from concourse import mybir

F32 = mybir.dt.float32
BF16 = mybir.dt.bfloat16
ALU = mybir.AluOpType
ACT = mybir.ActivationFunctionType
AX = mybir.AxisListType

P = 128
D = 128
W = 32
NA, NC = 4, 4
LC = 2
HD = 8
NL = 64
B, S = 2, 1024
CHUNK = S // NL
TOK = B * S
TILES = TOK // P
BPT = P // W
GT = 4
GROUPS = TILES // GT
GN = GT * P
TPB = S // P
GPB = TPB // GT
GL = GN // CHUNK
HID = 512
M = HID // P
RING = 3
NEG = -1.0e30
EPS = 1e-5
QK_SCALE = 1.0 / float(np.sqrt(HD))

C_ID, C_WIN, C_WIN0 = 0, 128, 192
C_LAT = 256
LATW = NL + 2 * (S // W - 1)
C_PATT = C_LAT + LATW
C_ONE = C_PATT + 128
C_CM = C_ONE + 32
C_LM = C_CM + NC
C_END = C_LM + LC


def latents(t):
    return GL * ((t // GT) % GPB + 1)


def constants():
    p = np.arange(P)
    a, q = p // 32, p % 32
    c = np.zeros((P, C_END), np.float32)
    c[:, C_ID:C_ID + 128] = np.eye(P)
    j = np.arange(2 * W)
    inside = (j[None] > q[:, None]) & (j[None] <= q[:, None] + W)
    c[:, C_WIN:C_WIN + 64] = np.where(inside, 0.0, NEG)
    c[:, C_WIN0:C_WIN0 + 64] = np.where(inside & (j[None] >= W), 0.0, NEG)
    u = np.arange(LATW) - 2 * (S // W - 1)
    c[:, C_LAT:C_LAT + LATW] = np.where(u[None] <= (q[:, None] // CHUNK), 0.0, NEG)
    cols = np.arange(P)
    same = (a[:, None] == (cols[None] // HD) % NA) & ((q // HD)[:, None] == cols[None] // 32)
    c[:, C_PATT:C_PATT + 128] = same
    c[:, C_ONE:C_ONE + 32] = a[:, None] == (np.arange(32)[None] // HD)
    c[:, C_CM:C_CM + NC] = (q // HD)[:, None] == np.arange(NC)[None]
    c[:, C_LM:C_LM + LC] = (q // HD)[:, None] == np.arange(LC)[None]
    return c


def ring_plan():
    order = []
    for step in steps():
        for part in step:
            if part[0] == "proj":
                order += [(n, part[1]) for n in ("q", "k", "gq", "gkv", "v", "zl", "zr")]
            elif part[0] == "ffn":
                order += ffn_uses(part[1], part[2], part[3])
    return {use: n for n, use in enumerate(order)}


def ffn_uses(g, stage, m):
    if stage == 0:
        return [("a", g, m), ("b", g, m)]
    if stage in (1, 2):
        return [(f"h{stage}", g, m)]
    return [("z", g)] if m == 0 else [("zt", g)] if m == 2 else []


def steps():
    out = [[("proj", 0)]]
    for t in range(TILES + GT + 1):
        parts = []
        if t < TILES:
            parts.append(("scores", t))
        if t < TILES and t % GT == GT - 1 and t // GT + 1 < GROUPS:
            parts.append(("proj", t // GT + 1))
        g, stage = (t - 1) // GT - 1, (t - 1) % GT
        unit = [("ffn", g, stage, m) for m in range(M)] if t >= 1 and 0 <= g < GROUPS else [("none",)] * M
        tail = [("pv", t - 1), ("rem", t - 1), ("y", t - 1), ("x1", t - 1)] if 1 <= t <= TILES else [("none",)] * M
        for u, v in zip(unit, tail):
            parts += [u, v]
        out.append([x for x in parts if x[0] != "none"])
    return out


def seq_block(nc, x_rows, x_cols, proj_w, gates_w, r_out_w, out_w, ffn_up, ffn_h1, ffn_h2, ffn_dn, scales, consts, out):
    plan = ring_plan()
    use_at = {n: use for use, n in plan.items()}
    order = steps()
    with ExitStack() as ctx:
        def sb(name, shape, dt=F32):
            return ctx.enter_context(nc.sbuf_tensor(name, shape, dt))

        def ps(name, shape):
            return ctx.enter_context(nc.psum_tensor(name, shape, F32))

        sems = {}

        def sem(name):
            if name not in sems:
                sems[name] = ctx.enter_context(nc.semaphore(name))
            return sems[name]

        scores_ps = ps("scores_ps", [P, 2, 512])
        lscores_ps = ps("lscores_ps", [P, BPT, LC, NL])
        pv_ps = ps("pv_ps", [P, 4, 128])
        mix_ps = ps("mix_ps", [P, 512])
        ring = [ps(f"ring{i}", [P, 512]) for i in range(RING)]

        cst = sb("cst", [P, C_END])
        xT = sb("xT", [P, TOK])
        xr = sb("xr", [P, TILES, D])
        wp = sb("wp", [P, 6, 128])
        gw = sb("gw", [P, 2])
        row = sb("row", [LC * 32, 128])
        wo = sb("wo", [P, 128])
        up = sb("up", [P, 2, HID])
        hw = [sb("hw1", [P, M, HID]), sb("hw2", [P, M, HID])]
        dn = sb("dn", [P, M, D])
        sc = sb("sc", [P, 4 * M + 1])
        idb = sb("idb", [P, 128], BF16)
        maskb = sb("maskb", [P, 128 + LATW], BF16)
        gpat = sb("gpat", [P, 2, 128])
        sc_t = sb("sc_t", [P, 2, M])
        negh = sb("negh", [P, 1])
        qa = [sb(f"qa{i}", [P, NA, GN]) for i in range(2)]
        gqa = [sb(f"gqa{i}", [P, NA, GN]) for i in range(2)]
        kc = [sb(f"kc{i}", [P, NC, W + GN]) for i in range(2)]
        vx = [sb(f"vx{i}", [P, GN // W, NC, NA, HD]) for i in range(2)]
        gate = [sb(f"gate{i}", [P, 2, GN]) for i in range(2)]
        qt = sb("qt", [P, GN])
        vt = sb("vt", [P, GN // W, NC, HD])
        xpool = sb("xpool", [P, GL])
        gvt = sb("gvt", [P, GL])
        gvr = sb("gvr", [P, 32])
        gkc = [sb(f"gkc{i}", [P, LC, NL]) for i in range(2)]
        gvx = [sb(f"gvx{i}", [P, NL // 32, LC, NA, HD]) for i in range(2)]
        mx = sb("mx", [P, BPT * NC])
        lmx = sb("lmx", [P, BPT * LC])
        pr = [sb(f"pr{i}", [P, BPT, NC, 2 * W]) for i in range(2)]
        lpr = [sb(f"lpr{i}", [P, BPT, LC, NL]) for i in range(2)]
        prT = sb("prT", [P, NC, BPT, 2 * W])
        lprT = sb("lprT", [P, LC, 2, BPT, 32])
        rden = sb("rden", [P, 128])
        rlden = sb("rlden", [64, 128])
        loc = sb("loc", [P, 128])
        remp = sb("remp", [64, 128])
        rmt = sb("rmt", [P, 128])
        comb = sb("comb", [P, 128])
        res = sb("res", [P, GT, D])
        st = sb("st", [P, GT, 6])
        mv = sb("mv", [P, GT, 2])
        ve = sb("ve", [P, GT])
        rs = sb("rs", [P, GT])
        x1 = [sb(f"x1_{i}", [P, GT, D]) for i in range(2)]
        x1T = [sb(f"x1T_{i}", [P, GN]) for i in range(2)]
        th = [sb(f"th{i}", [P, GN]) for i in range(2)]
        t1 = [sb(f"t1_{i}", [P, GN]) for i in range(2)]
        hid = [sb(f"hid{i}", [P, M, GN]) for i in range(3)]
        zs = sb("zs", [P, GN])
        res2 = sb("res2", [P, GT, D])
        st2 = sb("st2", [P, GT, 6])
        mv2 = sb("mv2", [P, GT, 2])
        ve2 = sb("ve2", [P, GT])
        rs2 = sb("rs2", [P, GT])
        fin = sb("fin", [P, GT, D])

        ident = cst[:, C_ID:C_ID + 128]
        ones_a = cst[:, C_ONE:C_ONE + 32]
        s_h = [sc[:, (2 + i) * M:(3 + i) * M] for i in range(2)]
        s_dn = sc[:, 4 * M:4 * M + 1]

        def bank(use):
            return ring[plan[use] % RING]

        def wait_full(eng, use):
            kind, g, *m = use
            eng.wait_ge(sem(f"{kind}_mm"), g * M + m[0] + 1 if m else g + 1)

        def wait_free(pe, use):
            n = plan[use] - RING
            if n < 0:
                return
            kind, g, *m = use_at[n]
            u = g * M + m[0] + 1 if m else g + 1
            readers = {
                "q": (("qa_ready", NA * u), ("qt_ready", u)),
                "gq": (("gqa_ready", NA * u),),
                "k": (("kc_ready", NC * u),),
                "gkv": (("gkc_ready", LC * u), ("gvt_ready", u)),
                "v": (("vt_ready", u),),
                "zl": (("gate_ready", 2 * u - 1),),
                "zr": (("gate_ready", 2 * u),),
                "a": (("t1_ready", u),),
                "b": (("hid0_ready", u),),
                "h1": (("hid1_ready", u),),
                "h2": (("hid2_ready", u),),
                "z": (("zs_ready", u),),
                "zt": (("res2_ready", GT * u),),
            }[kind]
            for name, value in readers:
                pe.wait_ge(sem(name), value)

        block = ctx.enter_context(nc.Block())

        @block.sync
        def _(sp):
            sp.dma_start(wp[:, :, :], proj_w).then_inc(sem("wp_in"), 16)
            sp.dma_start(xT[:, 0:GN], x_cols[:, 0:GN]).then_inc(sem("xT_in0"), 16)
            sp.dma_start(cst[:, :], consts).then_inc(sem("cst_in"), 16)
            for g in range(1, GROUPS):
                sp.dma_start(xT[:, g * GN:(g + 1) * GN], x_cols[:, g * GN:(g + 1) * GN]).then_inc(sem(f"xT_in{g}"), 16)
            for i, (w, src) in enumerate(((up, ffn_up), (hw[0], ffn_h1), (hw[1], ffn_h2), (dn, ffn_dn))):
                sp.dma_start(w[:, :, :], src).then_inc(sem(f"ffn_w_in{i}"), 16)
            for g in range(GROUPS):
                sp.wait_ge(sem("fin_ready"), GT * (g + 1))
                sp.dma_start(out.rearrange("(t p) d -> p t d", p=P)[:, g * GT:(g + 1) * GT, :],
                             fin[:, :, :]).then_inc(sem("out_done"), 16)
            sp.wait_ge(sem("out_done"), 16 * GROUPS)

        @block.gpsimd
        def _(pool):
            pool.dma_start(gw[:, :], gates_w).then_inc(sem("gw_in"), 16)
            pool.dma_start(row[:, :], r_out_w).then_inc(sem("row_in"), 16)
            pool.dma_start(wo[:, :], out_w).then_inc(sem("wo_in"), 16)
            pool.dma_start(sc[:, :], scales).then_inc(sem("sc_in"), 16)
            pool.dma_start(xr[:, :, :], x_rows.rearrange("(t p) d -> p t d", p=P)).then_inc(sem("xr_in"), 16)
            for i in range(2):
                pool.memset(vx[i][:, :, :, :, :], 0.0).then_inc(sem("vx_zero"), 1)
            pool.memset(negh[:, :], -0.5).then_inc(sem("negh_set"), 1)

            def spread_v(g):
                if g % GPB:
                    pool.wait_ge(sem("kc_ready"), NC * g)
                    if g >= 2:
                        pool.wait_ge(sem("scores_done"), GT * (g - 1))
                    pool.tensor_copy(kc[g % 2][:, :, 0:W], kc[(g - 1) % 2][:, :, GN:GN + W]).then_inc(sem("k_front"), 1)
                pool.wait_ge(sem("vt_ready"), g + 1)
                if g == 0:
                    pool.wait_ge(sem("vx_zero"), 2)
                    pool.wait_ge(sem("negh_set"), 1)
                if g % GPB:
                    pool.wait_ge(sem("k_front"), g // GPB + 1)
                if g >= 2:
                    pool.wait_ge(sem("pv_done"), GT * (g - 1) + 1)
                for a in range(NA):
                    r = slice(32 * a, 32 * a + 32)
                    if g or a:
                        pool.wait_ge(sem("vx_ready"), NA * g + a)
                    pool.tensor_copy(vx[g % 2][r, :, :, a, :], vt[r, :, :, :]).then_inc(sem("vx_ready"), 1)
                pool.wait_ge(sem("vx_ready"), NA * (g + 1))

            def rstd(t, var, power, rec, signal, first):
                pool.wait_ge(sem(var), t + 1)
                if first:
                    pool.wait_ge(sem("negh_set"), 1)
                i = t % GT
                pool.tensor_tensor(rec[:, i:i + 1], power[:, i:i + 1], negh[:, :], ALU.pow).then_inc(sem(signal), 1)

            for step in order:
                for kind, *at in step:
                    if kind == "proj":
                        spread_v(at[0])
                    elif kind == "y":
                        rstd(at[0], "var_ready", ve, rs, "rstd_ready", at[0] == 0)
                    elif kind == "ffn" and at[1:] == [3, 3]:
                        for i in range(GT):
                            rstd(at[0] * GT + i, "var2_ready", ve2, rs2, "rstd2_ready", False)

        @block.scalar
        def _(act):
            def proj(g):
                p = g % 2
                wait_full(act, ("q", g))
                if g == 0:
                    act.wait_ge(sem("q_zero"), 4)
                if g >= 2:
                    act.wait_ge(sem("scores_done"), GT * (g - 1))
                for a in range(NA):
                    r = slice(32 * a, 32 * a + 32)
                    act.activation(qa[p][r, a, :], bank(("q", g))[r, :], ACT.Copy, scale=QK_SCALE).then_inc(sem("qa_ready"), 1)
                if g >= 1:
                    act.wait_ge(sem("zr_mm"), g)
                act.activation(qt[:, :], bank(("q", g))[:, :], ACT.Copy).then_inc(sem("qt_ready"), 1)
                wait_full(act, ("gq", g))
                if g >= 2:
                    act.wait_ge(sem("lscores_done"), GT * (g - 1))
                for a in range(NA):
                    r = slice(32 * a, 32 * a + 32)
                    act.activation(gqa[p][r, a, :], bank(("gq", g))[r, :], ACT.Copy, scale=QK_SCALE).then_inc(sem("gqa_ready"), 1)
                if g >= 2:
                    act.wait_ge(sem("comb_ready"), GT * (g - 1))
                for i, z in enumerate(("zl", "zr")):
                    wait_full(act, (z, g))
                    act.activation(gate[p][:, i, :], bank((z, g))[:, :], ACT.Tanh, scale=0.5).then_inc(sem("gate_ready"), 1)

            def softmax(t):
                act.wait_ge(sem("sub_ready"), t + 1)
                v = pr[t % 2][:, :, :, :]
                act.activation(v, v, ACT.Exp).then_inc(sem("exp_ready"), 1)
                act.wait_ge(sem("lsub_ready"), t + 1)
                v = lpr[t % 2][:, :, :, 0:latents(t)]
                act.activation(v, v, ACT.Exp).then_inc(sem("lexp_ready"), 1)

            def ffn(g, stage, m):
                if stage == 0:
                    u = g * M + m
                    wait_full(act, ("a", g, m))
                    if u == 0:
                        act.wait_ge(sem("sct_ready"), 2)
                    if u >= 2:
                        act.wait_ge(sem("t1_ready"), u - 1)
                    act.activation(th[u % 2][:, :], bank(("a", g, m))[:, :], ACT.Tanh,
                                   scale=sc_t[:, 0, m:m + 1]).then_inc(sem("th_ready"), 1)
                elif stage in (1, 2):
                    wait_full(act, (f"h{stage}", g, m))
                    if g >= 1 and m == 0:
                        if stage == 1:
                            act.wait_ge(sem("h2_mm"), M * g)
                        else:
                            act.wait_ge(sem("z_mm"), g)
                    act.activation(hid[stage][:, m, :], bank((f"h{stage}", g, m))[:, :], ACT.Gelu,
                                   scale=s_h[stage - 1][:, m:m + 1]).then_inc(sem(f"hid{stage}_ready"), 1)
                elif m == 0:
                    wait_full(act, ("z", g))
                    if g >= 1:
                        act.wait_ge(sem("zt_mm"), g)
                    act.activation(zs[:, :], bank(("z", g))[:, :], ACT.Copy, scale=s_dn).then_inc(sem("zs_ready"), 1)

            def x1_cols(t):
                g, i = t // GT, t % GT
                act.wait_ge(sem("x1t_mm"), t + 1)
                if i == 0 and g >= 2:
                    act.wait_ge(sem("b_mm"), M * (g - 1))
                act.activation(x1T[g % 2][:, i * P:(i + 1) * P], mix_ps[:, 0:P], ACT.Copy).then_inc(sem("x1T_ready"), 1)

            act.wait_ge(sem("sc_in"), 16)
            for step in order:
                for kind, *at in step:
                    if kind == "proj":
                        proj(*at)
                    elif kind == "scores":
                        softmax(*at)
                    elif kind == "ffn":
                        ffn(*at)
                    elif kind == "x1":
                        x1_cols(*at)

        @block.vector
        def _(dve):
            def constants_on_chip():
                for i in range(2):
                    dve.memset(qa[i][:, :, :], 0.0).then_inc(sem("q_zero"), 1)
                    dve.memset(gqa[i][:, :, :], 0.0).then_inc(sem("q_zero"), 1)
                dve.memset(kc[0][:, :, 0:W], 0.0).then_inc(sem("k_zero"), 1)
                for i in range(2):
                    dve.memset(gvx[i][:, :, :, :, :], 0.0).then_inc(sem("l_zero"), 1)
                dve.wait_ge(sem("cst_in"), 16)
                dve.tensor_copy(idb[:, :], ident).then_inc(sem("masks_ready"), 1)
                dve.tensor_copy(maskb[:, :], cst[:, C_WIN:C_LAT + LATW]).then_inc(sem("masks_ready"), 1)
                dve.wait_ge(sem("gw_in"), 16)
                for i in range(2):
                    dve.tensor_scalar(gpat[:, i, :], cst[:, C_PATT:C_PATT + 128], gw[:, i:i + 1], None,
                                      ALU.mult).then_inc(sem("gpat_ready"), 1)
                dve.wait_ge(sem("sc_in"), 16)
                dve.tensor_scalar(sc_t[:, 0, :], sc[:, 0:M], 0.5, None, ALU.mult).then_inc(sem("sct_ready"), 1)
                dve.wait_ge(sem("sct_ready"), 1)
                dve.tensor_tensor(sc_t[:, 1, :], sc_t[:, 0, :], sc[:, M:2 * M], ALU.mult).then_inc(sem("sct_ready"), 1)

            def pool_x(g):
                dve.wait_ge(sem(f"xT_in{g}"), 16)
                if g >= 1:
                    dve.wait_ge(sem("gkv_mm"), g)
                dve.tensor_reduce(xpool[:, :], xT[:, g * GN:(g + 1) * GN].rearrange("p (n c) -> p n c", c=CHUNK),
                                  AX.X, ALU.add).then_inc(sem("xpool_ready"), 1)

            def proj(g):
                p = g % 2
                wait_full(dve, ("k", g))
                if g >= 2:
                    dve.wait_ge(sem("scores_done"), GT * (g - 1))
                    dve.wait_ge(sem("k_front"), g // GPB)
                for c in range(NC):
                    dve.tensor_scalar(kc[p][:, c, W:W + GN], bank(("k", g))[:, :], cst[:, C_CM + c:C_CM + c + 1], None,
                                      ALU.mult).then_inc(sem("kc_ready"), 1)
                b, n0 = g // GPB, (g % GPB) * GL
                wait_full(dve, ("gkv", g))
                if g == 0:
                    dve.wait_ge(sem("l_zero"), 2)
                for c in range(LC):
                    dve.tensor_scalar(gkc[b % 2][:, c, n0:n0 + GL], bank(("gkv", g))[:, 0:GL],
                                      cst[:, C_LM + c:C_LM + c + 1], 1.0 / CHUNK, ALU.mult, ALU.mult).then_inc(sem("gkc_ready"), 1)
                if g >= 1:
                    dve.wait_ge(sem("gvr_ready"), g)
                dve.tensor_scalar(gvt[:, :], bank(("gkv", g))[:, GL:2 * GL], 1.0 / CHUNK, None, ALU.mult).then_inc(sem("gvt_ready"), 1)
                dve.wait_ge(sem("gvt_ready"), g + 1)
                if g >= 1:
                    dve.wait_ge(sem("gvx_ready"), NA * g)
                dve.transpose(gvr[:, :], gvt[:, :]).then_inc(sem("gvr_ready"), 1)
                dve.wait_ge(sem("gvr_ready"), g + 1)
                for a in range(NA):
                    r = slice(32 * a, 32 * a + 32)
                    dve.tensor_copy(gvx[b % 2][r, n0 // 32, :, a, :],
                                    gvr[r, 0:LC * HD].rearrange("p (c d) -> p c d", c=LC)).then_inc(sem("gvx_ready"), 1)
                wait_full(dve, ("v", g))
                if g >= 1:
                    dve.wait_ge(sem("vx_ready"), NA * g)
                dve.transpose(vt[:, :, :, :].rearrange("p b c d -> p (b c d)"), bank(("v", g))[:, :]).then_inc(sem("vt_ready"), 1)
                if g + 1 < GROUPS:
                    pool_x(g + 1)

            def shift(t):
                s = scores_ps[:, :, :].rearrange("p k (r j) -> p (k r) j", j=2 * W)
                dve.wait_ge(sem("scores_done"), t + 1)
                if t >= 1:
                    dve.wait_ge(sem("sub_ready"), t)
                dve.tensor_reduce(mx[:, :], s, AX.X, ALU.max).then_inc(sem("max_ready"), 1)
                dve.wait_ge(sem("max_ready"), t + 1)
                if t >= 2:
                    dve.wait_ge(sem("prT_ready"), t - 1)
                dve.tensor_tensor(pr[t % 2][:, :, :, :].rearrange("p b c j -> p (b c) j"), s,
                                  mx[:, :].unsqueeze(2).to_broadcast([P, BPT * NC, 2 * W]), ALU.subtract).then_inc(sem("sub_ready"), 1)
                n = latents(t)
                s = lscores_ps[:, :, :, 0:n].rearrange("p b c n -> p (b c) n")
                dve.wait_ge(sem("lscores_done"), t + 1)
                if t >= 1:
                    dve.wait_ge(sem("lsub_ready"), t)
                dve.tensor_reduce(lmx[:, :], s, AX.X, ALU.max).then_inc(sem("lmax_ready"), 1)
                dve.wait_ge(sem("lmax_ready"), t + 1)
                if t >= 2:
                    dve.wait_ge(sem("lprT_ready"), t - 1)
                dve.tensor_tensor(lpr[t % 2][:, :, :, 0:n].rearrange("p b c n -> p (b c) n"), s,
                                  lmx[:, :].unsqueeze(2).to_broadcast([P, BPT * LC, n]), ALU.subtract).then_inc(sem("lsub_ready"), 1)

            def turn(t):
                dve.wait_ge(sem("exp_ready"), t + 1)
                if t >= 1:
                    dve.wait_ge(sem("pv_done"), t)
                dve.transpose(prT[:, :, :, :].rearrange("p c b j -> p b c j"), pr[t % 2][:, :, :, :]).then_inc(sem("prT_ready"), 1)
                dve.wait_ge(sem("lexp_ready"), t + 1)
                if t >= 1:
                    dve.wait_ge(sem("lpv_done"), t)
                n = latents(t) // 32
                for c in range(LC):
                    dve.transpose(lprT[:, c, 0:n, :, :].rearrange("p n b q -> p b n q"),
                                  lpr[t % 2][:, :, c, 0:32 * n].rearrange("p b (n j) -> p b n j", j=32)).then_inc(sem("lprT_ready"), 1)

            def weigh(t):
                dve.wait_ge(sem("lpv_done"), t + 1)
                if t >= 1:
                    dve.wait_ge(sem("remp_ready"), t)
                dve.reciprocal(rlden[:, :], pv_ps[64:128, 2, :]).then_inc(sem("rlden_ready"), 1)
                dve.wait_ge(sem("rlden_ready"), t + 1)
                if t >= 1:
                    dve.wait_ge(sem("rem_mm"), t)
                dve.tensor_tensor(remp[:, :], pv_ps[0:64, 2, :], rlden[:, :], ALU.mult).then_inc(sem("remp_ready"), 1)
                if t >= 1:
                    dve.wait_ge(sem("loc_ready"), 2 * t)
                dve.reciprocal(rden[:, :], pv_ps[:, 1, :]).then_inc(sem("rden_ready"), 1)
                dve.wait_ge(sem("rden_ready"), t + 1)
                if t >= 1:
                    dve.wait_ge(sem("comb_ready"), t)
                dve.tensor_tensor(loc[:, :], pv_ps[:, 0, :], rden[:, :], ALU.mult).then_inc(sem("loc_ready"), 1)
                dve.wait_ge(sem("loc_ready"), 2 * t + 1)
                g, i = t // GT, t % GT
                dve.wait_ge(sem("gate_ready"), 2 * (g + 1))
                cols = slice(i * P, (i + 1) * P)
                dve.scalar_tensor_tensor(out=loc[:, :], in0=gate[g % 2][:, 0, cols], scalar=1.0, in1=loc[:, :],
                                         op0=ALU.add, op1=ALU.mult).then_inc(sem("loc_ready"), 1)

            def combine(t):
                g, i = t // GT, t % GT
                cols = slice(i * P, (i + 1) * P)
                dve.wait_ge(sem("rem_mm"), t + 1)
                if t >= 1:
                    dve.wait_ge(sem("comb_ready"), t)
                dve.scalar_tensor_tensor(out=rmt[:, :], in0=gate[g % 2][:, 1, cols], scalar=1.0, in1=mix_ps[:, 0:P],
                                         op0=ALU.add, op1=ALU.mult).then_inc(sem("rmt_ready"), 1)
                dve.wait_ge(sem("rmt_ready"), t + 1)
                dve.wait_ge(sem("loc_ready"), 2 * t + 2)
                if t >= 1:
                    dve.wait_ge(sem("y_mm"), t)
                dve.tensor_tensor(comb[:, :], loc[:, :], rmt[:, :], ALU.add).then_inc(sem("comb_ready"), 1)

            def norm(t, r, stats, mean_var, power, rec, dst, before, after):
                i = t % GT
                dve.wait_ge(sem(before), t + 1)
                dve.bn_stats(stats[:, i, :], r[:, i, :]).then_inc(sem(f"{after}_stats"), 1)
                dve.wait_ge(sem(f"{after}_stats"), t + 1)
                dve.bn_aggr(mean_var[:, i, :], stats[:, i, :]).then_inc(sem(f"{after}_aggr"), 1)
                dve.wait_ge(sem(f"{after}_aggr"), t + 1)
                dve.tensor_scalar(power[:, i:i + 1], mean_var[:, i, 1:2], EPS, None, ALU.add).then_inc(
                    sem("var_ready" if after == "x1" else "var2_ready"), 1)

            def scale_rows(t, r, mean_var, rec, dst, ready, signal):
                i = t % GT
                dve.wait_ge(sem(ready), t + 1)
                dve.tensor_scalar(dst[:, i, :], r[:, i, :], mean_var[:, i, 0:1], rec[:, i:i + 1],
                                  ALU.subtract, ALU.mult).then_inc(sem(signal), 1)

            def first_norm(t):
                g, i = t // GT, t % GT
                dve.wait_ge(sem("y_mm"), t + 1)
                if t == 0:
                    dve.wait_ge(sem("xr_in"), 16)
                if t >= GT:
                    dve.wait_ge(sem("x1_ready"), t - GT + 1)
                dve.scalar_tensor_tensor(out=res[:, i, :], in0=mix_ps[:, 0:D], scalar=0.5, in1=xr[:, t, :],
                                         op0=ALU.mult, op1=ALU.add).then_inc(sem("res_ready"), 1)
                norm(t, res, st, mv, ve, rs, None, "res_ready", "x1")
                if g >= 2 and i == 0:
                    dve.wait_ge(sem("res2_ready"), GT * (g - 1))
                scale_rows(t, res, mv, rs, x1[g % 2], "rstd_ready", "x1_ready")

            def ffn(g, stage, m):
                if stage == 0:
                    u = g * M + m
                    wait_full(dve, ("a", g, m))
                    dve.wait_ge(sem("th_ready"), u + 1)
                    if u >= 2:
                        dve.wait_ge(sem("hid0_ready"), u - 1)
                    dve.scalar_tensor_tensor(out=t1[u % 2][:, :], in0=th[u % 2][:, :], scalar=1.0, in1=bank(("a", g, m))[:, :],
                                             op0=ALU.add, op1=ALU.mult).then_inc(sem("t1_ready"), 1)
                    wait_full(dve, ("b", g, m))
                    dve.wait_ge(sem("t1_ready"), u + 1)
                    dve.wait_ge(sem("sct_ready"), 2)
                    if g >= 1 and m == 0:
                        dve.wait_ge(sem("h1_mm"), M * g)
                    dve.scalar_tensor_tensor(out=hid[0][:, m, :], in0=bank(("b", g, m))[:, :], scalar=sc_t[:, 1, m:m + 1],
                                             in1=t1[u % 2][:, :], op0=ALU.mult, op1=ALU.mult).then_inc(sem("hid0_ready"), 1)
                elif stage == 3 and m == 3:
                    wait_full(dve, ("zt", g))
                    for i in range(GT):
                        t = g * GT + i
                        if g >= 1:
                            dve.wait_ge(sem("fin_ready"), t - GT + 1)
                        dve.tensor_tensor(res2[:, i, :], bank(("zt", g))[:, i * P:(i + 1) * P], x1[g % 2][:, i, :],
                                          ALU.add).then_inc(sem("res2_ready"), 1)
                    for i in range(GT):
                        norm(g * GT + i, res2, st2, mv2, ve2, rs2, None, "res2_ready", "x2")
                    if g >= 1:
                        dve.wait_ge(sem("out_done"), 16 * g)
                    for i in range(GT):
                        scale_rows(g * GT + i, res2, mv2, rs2, fin, "rstd2_ready", "fin_ready")

            constants_on_chip()
            pool_x(0)
            for step in order:
                for kind, *at in step:
                    if kind == "proj":
                        proj(*at)
                    elif kind == "scores":
                        shift(*at)
                    elif kind == "ffn":
                        ffn(*at)
                    elif kind == "pv":
                        weigh(*at)
                    elif kind == "rem":
                        combine(*at)
                    elif kind == "y":
                        first_norm(*at)
                for kind, *at in step:
                    if kind == "scores":
                        turn(*at)

        @block.tensor
        def _(pe):
            def proj(g):
                cols = xT[:, g * GN:(g + 1) * GN]
                pe.wait_ge(sem(f"xT_in{g}"), 16)
                for kind, w, src in (("q", 0, cols), ("k", 1, cols), ("gq", 3, cols), ("gkv", 4, xpool[:, :]), ("v", 2, cols)):
                    wait_free(pe, (kind, g))
                    o = bank((kind, g))
                    if kind == "gkv":
                        pe.wait_ge(sem("xpool_ready"), g + 1)
                        pe.matmul(o[:, 0:GL], wp[:, 4, :], src, start=True, stop=True)
                        i = pe.matmul(o[:, GL:2 * GL], wp[:, 5, :], src, start=True, stop=True)
                    else:
                        i = pe.matmul(o[:, :], wp[:, w, :], src, start=True, stop=True)
                    i.then_inc(sem(f"{kind}_mm"), 1)
                pe.wait_ge(sem("qt_ready"), g + 1)
                if g == 0:
                    pe.wait_ge(sem("gpat_ready"), 2)
                for i, kind in enumerate(("zl", "zr")):
                    wait_free(pe, (kind, g))
                    pe.matmul(bank((kind, g))[:, :], gpat[:, i, :], qt[:, :], start=True, stop=True).then_inc(sem(f"{kind}_mm"), 1)

            def scores(t):
                g, i = t // GT, t % GT
                p = g % 2
                if t == 0:
                    pe.wait_ge(sem("masks_ready"), 2)
                    pe.wait_ge(sem("k_zero"), 1)
                if t >= 1:
                    pe.wait_ge(sem("sub_ready"), t)
                if i == 0:
                    pe.wait_ge(sem("qa_ready"), NA * (g + 1))
                    pe.wait_ge(sem("kc_ready"), NC * (g + 1))
                    if g % GPB:
                        pe.wait_ge(sem("k_front"), g // GPB + 1)
                first = t % TPB == 0
                for k in range(2):
                    if k == 0 and first:
                        for b in range(2):
                            m = maskb[:, 64 * (1 - b):64 * (1 - b) + 64].unsqueeze(1).to_broadcast([P, NC, 2 * W])
                            pe.matmul(scores_ps[:, 0, 256 * b:256 * b + 256], idb[:, :], m, start=(b == 0), stop=False,
                                      skip_group_check=True)
                    else:
                        m = maskb[:, 0:64].unsqueeze(1).to_broadcast([P, 2 * NC, 2 * W])
                        pe.matmul(scores_ps[:, k, :], idb[:, :], m, start=True, stop=False, skip_group_check=True)
                    for b in range(2):
                        w = (i * BPT + 2 * k + b) * W
                        for a in range(NA):
                            mm = pe.matmul(scores_ps[32 * a:32 * a + 32, k, 256 * b:256 * b + 256], qa[p][:, a, w:w + W],
                                           kc[p][:, :, w:w + 2 * W], start=False, stop=True, skip_group_check=True)
                mm.then_inc(sem("scores_done"), 1)
                if t >= 1:
                    pe.wait_ge(sem("lsub_ready"), t)
                if i == 0:
                    pe.wait_ge(sem("gqa_ready"), NA * (g + 1))
                    pe.wait_ge(sem("gkc_ready"), LC * (g + 1))
                n = latents(t)
                for b in range(BPT):
                    u = 2 * (S // W - 1) - 2 * ((t % TPB) * BPT + b)
                    m = maskb[:, 128 + u:128 + u + n].unsqueeze(1).to_broadcast([P, LC, n])
                    pe.matmul(lscores_ps[:, b, :, 0:n], idb[:, :], m, start=(b == 0), stop=False, skip_group_check=True)
                for b in range(BPT):
                    w = (i * BPT + b) * W
                    for a in range(NA):
                        mm = pe.matmul(lscores_ps[32 * a:32 * a + 32, b, :, 0:n], gqa[p][:, a, w:w + W],
                                       gkc[(g // GPB) % 2][:, :, 0:n], start=False, stop=True, skip_group_check=True)
                mm.then_inc(sem("lscores_done"), 1)

            def pv(t):
                g, i = t // GT, t % GT
                pe.wait_ge(sem("prT_ready"), t + 1)
                if i == 0:
                    pe.wait_ge(sem("vx_ready"), NA * (g + 1))
                if t >= 1:
                    pe.wait_ge(sem("remp_ready"), t)
                    pe.wait_ge(sem("loc_ready"), 2 * t)
                flat = prT[:, :, :, :].rearrange("p c b j -> p c (b j)")
                for kb in range(-1, BPT):
                    if kb < 0 and t % TPB == 0:
                        continue
                    lo, hi = max(0, kb * 64 + 32), min(256, kb * 64 + 96)
                    if kb < 0:
                        v = vx[g % 2][:, i * BPT - 1] if i else vx[(g - 1) % 2][:, GN // W - 1]
                        lo, hi = 0, 32
                    else:
                        v = vx[g % 2][:, i * BPT + kb]
                    q0 = 32 * max(kb, 0)
                    for c in range(NC):
                        pe.matmul(pv_ps[32 * c:32 * c + 32, 0, q0:q0 + hi - lo], v[:, c, :, :], flat[:, c, lo:hi],
                                  start=(kb == -1 or (kb == 0 and t % TPB == 0)), stop=True, skip_group_check=True)
                halves = prT[:, :, :, :].rearrange("p c b (h q) -> p c h b q", h=2)
                for h in range(2):
                    for c in range(NC):
                        mm = pe.matmul(pv_ps[32 * c:32 * c + 32, 1, :], ones_a, halves[:, c, h, :, :],
                                       start=False, stop=True, skip_group_check=True)
                mm.then_inc(sem("pv_done"), 1)
                pe.wait_ge(sem("lprT_ready"), LC * (t + 1))
                if i == 0:
                    pe.wait_ge(sem("gvx_ready"), NA * (g + 1))
                for n in range(latents(t) // 32):
                    for c in range(LC):
                        r = lprT[:, c, n, :, :].rearrange("p b q -> p (b q)")
                        pe.matmul(pv_ps[32 * c:32 * c + 32, 2, :], gvx[(g // GPB) % 2][:, n, c, :, :], r,
                                  start=False, stop=True, skip_group_check=True)
                        mm = pe.matmul(pv_ps[64 + 32 * c:96 + 32 * c, 2, :], ones_a, r,
                                       start=False, stop=True, skip_group_check=True)
                mm.then_inc(sem("lpv_done"), 1)

            def remote(t):
                if t == 0:
                    pe.wait_ge(sem("row_in"), 16)
                else:
                    pe.wait_ge(sem("x1T_ready"), t)
                pe.wait_ge(sem("remp_ready"), t + 1)
                pe.matmul(mix_ps[:, 0:P], row[:, :], remp[:, :], start=True, stop=True).then_inc(sem("rem_mm"), 1)

            def y(t):
                if t == 0:
                    pe.wait_ge(sem("wo_in"), 16)
                pe.wait_ge(sem("rmt_ready"), t + 1)
                pe.wait_ge(sem("comb_ready"), t + 1)
                pe.matmul(mix_ps[:, 0:D], comb[:, :], wo[:, :], start=True, stop=True).then_inc(sem("y_mm"), 1)

            def x1_turn(t):
                pe.wait_ge(sem("res_ready"), t + 1)
                pe.wait_ge(sem("x1_ready"), t + 1)
                pe.transpose(mix_ps[:, 0:P], x1[(t // GT) % 2][:, t % GT, :], ident).then_inc(sem("x1t_mm"), 1)

            def ffn(g, stage, m):
                if stage == 0:
                    if m == 0:
                        pe.wait_ge(sem("x1T_ready"), GT * (g + 1))
                        pe.wait_ge(sem("ffn_w_in0"), 16)
                    for i, kind in enumerate("ab"):
                        wait_free(pe, (kind, g, m))
                        pe.matmul(bank((kind, g, m))[:, :], up[:, i, m * P:(m + 1) * P], x1T[g % 2][:, :],
                                  start=True, stop=True).then_inc(sem(f"{kind}_mm"), 1)
                elif stage in (1, 2):
                    if m == 0:
                        pe.wait_ge(sem(f"ffn_w_in{stage}"), 16)
                    use = (f"h{stage}", g, m)
                    wait_free(pe, use)
                    for k in range(M):
                        if m == 0:
                            pe.wait_ge(sem(f"hid{stage - 1}_ready"), g * M + k + 1)
                        mm = pe.matmul(bank(use)[:, :], hw[stage - 1][:, k, m * P:(m + 1) * P], hid[stage - 1][:, k, :],
                                       start=(k == 0), stop=(k == M - 1))
                    mm.then_inc(sem(f"h{stage}_mm"), 1)
                elif m == 0:
                    pe.wait_ge(sem("ffn_w_in3"), 16)
                    wait_free(pe, ("z", g))
                    for k in range(M):
                        pe.wait_ge(sem("hid2_ready"), g * M + k + 1)
                        mm = pe.matmul(bank(("z", g))[:, :], dn[:, k, :], hid[2][:, k, :], start=(k == 0), stop=(k == M - 1))
                    mm.then_inc(sem("z_mm"), 1)
                elif m == 2:
                    pe.wait_ge(sem("zs_ready"), g + 1)
                    wait_free(pe, ("zt", g))
                    for i in range(GT):
                        mm = pe.transpose(bank(("zt", g))[:, i * P:(i + 1) * P], zs[:, i * P:(i + 1) * P], ident)
                    mm.then_inc(sem("zt_mm"), 1)

            pe.wait_ge(sem("wp_in"), 16)
            for step in order:
                for kind, *at in step:
                    if kind == "proj":
                        proj(*at)
                    elif kind == "scores":
                        scores(*at)
                    elif kind == "ffn":
                        ffn(*at)
                    elif kind == "pv":
                        pv(*at)
                    elif kind == "rem":
                        remote(*at)
                    elif kind == "y":
                        y(*at)
                    elif kind == "x1":
                        x1_turn(*at)


def kernel(**inputs):
    import concourse.bacc as bacc
    from concourse.bass_utils import run_bass_kernel_spmd

    f = {k: np.asarray(v) for k, v in inputs.items()}
    x = f["L0_attn_x"].reshape(TOK, D)

    def pad(w):
        o = np.zeros((D, NA, 32), w.dtype)
        o[:, :, 0:LC * HD] = w.reshape(D, NA, LC * HD)
        return o.reshape(D, 128)

    def rows(w, n):
        return w.reshape(NA, n, HD, -1).transpose(1, 0, 2, 3).reshape(NA * n * HD, -1)

    def up(w):
        return w.T

    def down(w):
        return w.T.reshape(M, P, -1).transpose(1, 0, 2)

    def col(v):
        return v.reshape(-1, P).T

    a, h = "L0_attn_", "L0_ffn_"
    arrays = {
        "x_rows": x,
        "x_cols": x.T,
        "proj_w": np.stack([f[a + "wq"], f[a + "wk"], f[a + "wv"]] + [pad(f[a + n]) for n in ("wgq", "wgk", "wgv")], 1),
        "gates_w": np.stack([f[a + "gate_local_w"].reshape(P), f[a + "gate_remote_w"].reshape(P)], 1),
        "r_out_w": rows(rows(f[a + "r_out_w"], LC).T, NC).T,
        "out_w": rows(f[a + "w_out"], NC),
        "ffn_up": np.stack([f[h + "w1_w"].T, f[h + "w2_w"].T], 1),
        "ffn_h1": down(f[h + "h1_w"]),
        "ffn_h2": down(f[h + "h2_w"]),
        "ffn_dn": down(f[h + "w3_w"]),
        "scales": np.concatenate([col(f[h + n]) for n in ("w1_s", "w2_s", "h1_s", "h2_s", "w3_s")], 1),
        "consts": constants(),
    }
    nc = bacc.Bacc("TRN2", target_bir_lowering=False, num_devices=1)
    arrays = {k: np.ascontiguousarray(v) for k, v in arrays.items()}
    args = [nc.dram_tensor(k, v.shape, mybir.dt.from_np(v.dtype), kind="ExternalInput").ap() for k, v in arrays.items()]
    args.append(nc.dram_tensor("out", (TOK, D), F32, kind="ExternalOutput").ap())
    seq_block(nc, *args)
    r = run_bass_kernel_spmd(nc, [arrays], core_ids=[0])
    return r.results[0]["out"].reshape(B, S, D)
```

```python
from contextlib import ExitStack

import numpy as np

import concourse.bass as bass
from concourse import mybir

F32 = mybir.dt.float32
BF16 = mybir.dt.bfloat16
F32R = mybir.dt.float32r
I32 = mybir.dt.int32
ALU = mybir.AluOpType
ACT = mybir.ActivationFunctionType
AX = mybir.AxisListType

P = 128
D = 128
W = 32
NA, NC = 4, 4
LC = 2
HD = 8
NL = 64
B, S = 2, 1024
CHUNK = S // NL
TOK = B * S
TILES = TOK // P
BPT = P // W
GT = 4
GROUPS = TILES // GT
GN = GT * P
TPB = S // P
GPB = TPB // GT
GL = GN // CHUNK
HID = 512
M = HID // P
FT = 2
FN = FT * P
FB = TILES // FT
RING = 3
NEG = -1.0e30
FFN_W = (2 * HID, M * HID, M * HID, M * D)
EPS = 1e-5
QK_SCALE = 1.0 / float(np.sqrt(HD))

C_ID, C_WIN, C_WIN0 = 0, 128, 192
C_LAT = 256
LATW = NL + 2 * (S // W - 1)
C_PATT = C_LAT + LATW
C_ONE = C_PATT + 128
C_CM = C_ONE + 32
C_LM = C_CM + NC
C_END = C_LM + LC


def latents(t):
    return GL * ((t // GT) % GPB + 1)


def constants():
    p = np.arange(P)
    a, q = p // 32, p % 32
    c = np.zeros((P, C_END), np.float32)
    c[:, C_ID:C_ID + 128] = np.eye(P)
    j = np.arange(2 * W)
    inside = (j[None] > q[:, None]) & (j[None] <= q[:, None] + W)
    c[:, C_WIN:C_WIN + 64] = np.where(inside, 0.0, NEG)
    c[:, C_WIN0:C_WIN0 + 64] = np.where(inside & (j[None] >= W), 0.0, NEG)
    u = np.arange(LATW) - 2 * (S // W - 1)
    c[:, C_LAT:C_LAT + LATW] = np.where(u[None] <= (q[:, None] // CHUNK), 0.0, NEG)
    cols = np.arange(P)
    same = (a[:, None] == (cols[None] // HD) % NA) & ((q // HD)[:, None] == cols[None] // 32)
    c[:, C_PATT:C_PATT + 128] = same
    c[:, C_ONE:C_ONE + 32] = a[:, None] == (np.arange(32)[None] // HD)
    c[:, C_CM:C_CM + NC] = (q // HD)[:, None] == np.arange(NC)[None]
    c[:, C_LM:C_LM + LC] = (q // HD)[:, None] == np.arange(LC)[None]
    return c


def ring_plan():
    order = []
    for kind, *at in work_of("PE"):
        if kind == "proj":
            order.append(tuple(at))
        elif kind == "flag":
            order.append(("flag", 0))
        elif kind == "ffn":
            f, stage, m = at
            if stage in (0, 3) or m % 2 == 0:
                order.append(ffn_use(f, stage, m))
    return {use: n for n, use in enumerate(order)}


def ffn_use(f, stage, m):
    if stage == 3:
        return ("z", f) if m == 0 else ("zt", f)
    return ("ab", f, m) if stage == 0 else (f"h{stage}", f, m // 2)


ORDER = {
    "PE": (
        [("proj", "q"), ("proj", "k"), ("proj", "gq"), ("scores", 0), ("proj", "gkv"), ("proj", "zl"),
         ("lscores", 0), ("proj", "v"), ("proj", "zr")],
        [("scores", 1), ("x1_turn", -1), ("ffn", 3, 3, 1), ("lscores", 1), ("ffn", 1, 0, 0), ("ffn", 1, 0, 1),
         ("ffn", 1, 0, 2), ("pv", 0), ("ffn", 1, 0, 3), ("lpv", 0), ("proj", "q"), ("ffn", 2, 2, 0),
         ("ffn", 2, 2, 1), ("rem", 0), ("proj", "k"), ("ffn", 2, 2, 2), ("ffn", 2, 2, 3), ("y", 0)],
        [("proj", "gq"), ("proj", "gkv"), ("scores", 1), ("ffn", 1, 1, 0), ("ffn", 1, 1, 1), ("x1_turn", -1),
         ("proj", "v"), ("lscores", 1), ("proj", "zl"), ("proj", "zr"), ("pv", 0), ("lpv", 0), ("ffn", 1, 1, 2),
         ("ffn", 1, 1, 3), ("rem", 0), ("ffn", 2, 3, 0), ("y", 0)],
    ),
    "ACT": (
        [("out", "qt"), ("out", "qa"), ("out", "gq")],
        [("exp", 0), ("x1_hi", -1), ("lexp", 0), ("silu", 1, 0), ("silu", 1, 1), ("silu", 1, 2), ("hi", 1, 0, 0),
         ("silu", 1, 3), ("hi", 1, 0, 1), ("out", "qa"), ("out", "qt"), ("gelu", 2, 2, 1), ("gelu", 2, 2, 0),
         ("hi", 2, 2, 0), ("gelu", 2, 2, 2), ("gelu", 2, 2, 3)],
        [("hi", 2, 2, 1), ("exp", 0), ("lexp", 0), ("out", "gq"), ("x1_hi", -1), ("gelu", 1, 1, 0),
         ("gelu", 1, 1, 1), ("hi", 1, 1, 0), ("out", "zl"), ("gelu", 1, 1, 3), ("out", "zr"), ("gelu", 1, 1, 2),
         ("hi", 1, 1, 1), ("zs", 2)],
    ),
    "DVE": (
        [("pool", "x0"), ("out", "k"), ("out", "gk"), ("max", 0), ("out", "gv"), ("sub", 0), ("pool", "x"),
         ("out", "v")],
        [("lmax", 0), ("lo", 2, 1, 1), ("res", -1), ("stats", -1), ("aggr", -1), ("eps", -1), ("lsub", 0),
         ("x1_rows", -1), ("turn", 0), ("x1_lo", -1), ("res2", 3), ("stats2", 3), ("aggr2", 3), ("lturn", 0),
         ("mul", 1, 0), ("eps2", 3), ("mul", 1, 1), ("mul", 1, 2), ("max", 1), ("mul", 1, 3), ("lrecip", 0),
         ("recip", 0), ("lweigh", 0), ("weigh", 0), ("sub", 1), ("gated", 0), ("rmt", 0), ("comb", 0), ("fin", 3),
         ("out", "k"), ("lo", 1, 0, 0), ("lo", 2, 2, 0), ("lo", 2, 2, 1), ("lo", 1, 0, 1)],
        [("res", -1), ("stats", -1), ("aggr", -1), ("lmax", 0), ("lsub", 0), ("eps", -1), ("out", "gk"),
         ("x1_rows", -1), ("out", "gv"), ("turn", 0), ("lturn", 0), ("pool", "x"), ("x1_lo", -1), ("out", "v"),
         ("max", 1), ("sub", 1), ("lrecip", 0), ("lweigh", 0), ("recip", 0), ("weigh", 0), ("gated", 0), ("rmt", 0),
         ("comb", 0), ("lo", 1, 1, 0)],
    ),
    "Pool": (
        [("front", "k"), ("split", 0), ("split", 1)],
        [("rstd", -1), ("rstd2", 3), ("lo", 1, 0, 0), ("lo", 1, 0, 1), ("front", "k"), ("lo", 2, 2, 0),
         ("lo", 2, 2, 1)],
        [("rstd", -1), ("lo", 1, 1, 0), ("lo", 1, 1, 1)],
    ),
}
BESIDES = {
    "PE": {2: [(1, "flag", 0)]},
    "ACT": {0: [(1, "out", "zl"), (2, "split", 0), (2, "split", 1), (4, "split", 2), (5, "out", "zr")], 1: [(2, "split", 3)]},
    "DVE": {0: [(14, "check", 0)], 1: [(8, "check", 1), (20, "check", 2)], 2: [(6, "check", 3), (7, "flag", 0)]},
    "Pool": {0: [(1, "split", 2)], 1: [(1, "split", 3)]},
}
FFN_KINDS = ("ffn", "silu", "mul", "gelu", "hi", "lo", "zs", "res2", "stats2", "aggr2", "eps2", "rstd2", "fin")
PROJ_KINDS = ("proj", "out", "front", "pool")


def work_of(engine):
    start, even, odd = ORDER[engine]
    out = [(kind, what, 0) if kind in PROJ_KINDS else (kind, what) for kind, what in start]
    for t in range(TILES + 6):
        entries = list((even, odd)[t % 2])
        besides = BESIDES[engine].get(t, [])
        for n, (after, kind, what) in enumerate(besides):
            entries.insert(after + n, ("besides", kind, what))
        for kind, at, *more in entries:
            if kind == "besides":
                out.append((at, *more, 0) if at in PROJ_KINDS else (at, *more))
                continue
            if kind in FFN_KINDS:
                f = t // 2 - at
                if 0 <= f < FB:
                    out.append((kind, f, *more))
            elif kind in PROJ_KINDS:
                if t % GT >= GT // 2 and t // GT + 1 < GROUPS:
                    out.append((kind, at, t // GT + 1))
            elif 0 <= t + at < TILES:
                out.append((kind, t + at))
    return out


def seq_block(nc, x_rows, x_cols, proj_w, gates_w, r_out_w, out_w, ffn_w0, ffn_w1, ffn_w2, ffn_w3, scales, consts, out):
    ffn_w = (ffn_w0, ffn_w1, ffn_w2, ffn_w3)
    plan = ring_plan()
    use_at = {n: use for use, n in plan.items()}
    with ExitStack() as ctx:
        def sb(name, shape, dt=F32):
            return ctx.enter_context(nc.sbuf_tensor(name, shape, dt))

        def ps(name, shape):
            return ctx.enter_context(nc.psum_tensor(name, shape, F32))

        sems = {}

        def sem(name):
            if name not in sems:
                sems[name] = ctx.enter_context(nc.semaphore(name))
            return sems[name]

        scores_ps = ps("scores_ps", [P, 2, 512])
        lscores_ps = ps("lscores_ps", [P, BPT, LC, NL])
        pv_ps = ps("pv_ps", [P, 4, 128])
        mix_ps = ps("mix_ps", [P, 512])
        ring = [ps(f"ring{i}", [P, 512]) for i in range(RING)]

        cst = sb("cst", [P, C_END])
        xT = [sb(f"xT{i}", [P, GN]) for i in range(2)]
        xr = [sb(f"xr{i}", [P, GT, D]) for i in range(2)]
        wp = sb("wp", [P, 6, 128])
        gw = sb("gw", [P, 2])
        row = sb("row", [LC * 32, 128])
        wo = sb("wo", [P, 128])
        wraw = [sb(f"wraw{i}", [P, max(FFN_W)]) for i in range(2)]
        w_hi = [sb(f"w_hi{i}", [P, n], F32R) for i, n in enumerate(FFN_W)]
        w_lo = [sb(f"w_lo{i}", [P, n], F32R) for i, n in enumerate(FFN_W)]
        w_max = sb("w_max", [P, len(FFN_W) + 1])
        flag_max = sb("flag_max", [1, 1])
        flag = sb("flag", [1, 1], I32)
        sc = sb("sc", [P, 4 * M + 1])
        idb = sb("idb", [P, 128], BF16)
        maskb = sb("maskb", [P, 128 + LATW], BF16)
        gpat = sb("gpat", [P, 2, 128])
        warm = sb("warm", [P, 2])
        negh = sb("negh", [P, FT])
        qa = sb("qa", [P, NA, GN])
        gqa = sb("gqa", [P, NA, GN])
        kc = sb("kc", [P, NC, W + GN])
        vx = [sb(f"vx{i}", [P, GN // W, NC, NA, HD]) for i in range(2)]
        gate = [sb(f"gate{i}", [P, 2, GN]) for i in range(2)]
        qt = sb("qt", [P, GN])
        xpool = sb("xpool", [P, GL])
        gvt = sb("gvt", [P, GL])
        gvr = sb("gvr", [P, 32])
        gkc = [sb(f"gkc{i}", [P, LC, NL]) for i in range(2)]
        gvx = [sb(f"gvx{i}", [P, NL // 32, LC, NA, HD]) for i in range(2)]
        mx = sb("mx", [P, BPT * NC])
        lmx = sb("lmx", [P, BPT * LC])
        pr = [sb(f"pr{i}", [P, BPT, NC, 2 * W]) for i in range(2)]
        lpr = [sb(f"lpr{i}", [P, BPT, LC, NL]) for i in range(2)]
        prT = sb("prT", [P, NC, BPT, 2 * W])
        lprT = sb("lprT", [P, LC, 2, BPT, 32])
        rden = sb("rden", [P, 128])
        rlden = sb("rlden", [64, 128])
        loc = sb("loc", [P, 128])
        remp = sb("remp", [64, 128])
        rmt = sb("rmt", [P, 128])
        comb = sb("comb", [P, 128])
        res = sb("res", [P, GT, D])
        st = sb("st", [P, GT, 6])
        mv = sb("mv", [P, GT, 2])
        ve = sb("ve", [P, GT])
        rs = sb("rs", [P, GT])
        x1 = [sb(f"x1_{i}", [P, GT, D]) for i in range(2)]
        x1_hi = sb("x1_hi", [P, GN], F32R)
        x1_lo = sb("x1_lo", [P, GN], F32R)
        silu = [sb(f"silu{i}", [P, FN]) for i in range(2)]
        hf = [sb(f"hf{i}", [P, M, FN]) for i in range(3)]
        h_hi = [sb(f"h_hi{i}", [P, M, FN], F32R) for i in range(3)]
        h_lo = [sb(f"h_lo{i}", [P, M, FN], F32R) for i in range(3)]
        zs = sb("zs", [P, FN])
        res2 = sb("res2", [P, FT, D])
        st2 = sb("st2", [P, FT, 6])
        mv2 = sb("mv2", [P, FT, 2])
        ve2 = sb("ve2", [P, FT])
        rs2 = sb("rs2", [P, FT])
        fin = [sb(f"fin{i}", [P, FT, D]) for i in range(2)]

        ident = cst[:, C_ID:C_ID + 128]
        ones_a = cst[:, C_ONE:C_ONE + 32]
        s_h = [sc[:, (2 + i) * M:(3 + i) * M] for i in range(2)]
        s_dn = sc[:, 4 * M:4 * M + 1]

        def bank(use):
            return ring[plan[use] % RING]

        def wait_full(eng, use):
            eng.wait_ge(sem(f"{use[0]}_mm"), number(use) + 1)

        def number(use):
            kind, g, *j = use
            return g * {"ab": M, "h1": 2, "h2": 2}[kind] + j[0] if j else g

        def wait_free(pe, use):
            n = plan[use] - RING
            if n < 0:
                return
            kind, g, *j = use_at[n]
            u = number(use_at[n]) + 1
            readers = {
                "q": (("qa_ready", NA * u), ("qt_ready", u)),
                "gq": (("gqa_ready", NA * u),),
                "k": (("kc_ready", NC * u),),
                "gkv": (("gkc_ready", LC * u), ("gvt_ready", u)),
                "v": (("vx_ready", NA * u),),
                "zl": (("gate_ready", 2 * u - 1),),
                "zr": (("gate_ready", 2 * u),),
                "ab": (("hidden0_ready", u),),
                "h1": (("hidden1_ready", 2 * u),),
                "h2": (("hidden2_ready", 2 * u),),
                "flag": (("flag_max_ready", 1),),
                "z": (("zs_ready", u),),
                "zt": (("res2_ready", u),),
            }[kind]
            for name, value in readers:
                pe.wait_ge(sem(name), value)

        block = ctx.enter_context(nc.Block())

        @block.sync
        def _(sp):
            def load_x_cols(g):
                if g >= 2:
                    sp.wait_ge(sem("v_mm"), g - 1)
                    sp.wait_ge(sem("xpool_ready"), g - 1)
                sp.dma_start(xT[g % 2][:, :], x_cols[:, g * GN:(g + 1) * GN]).then_inc(sem(f"xT_in{g % 2}"), 16)

            def load_x_rows(g):
                if g >= 2:
                    sp.wait_ge(sem("res_ready"), GT * (g - 1))
                sp.dma_start(xr[g % 2][:, :, :], x_rows.rearrange("(t p) d -> p t d", p=P)[:, g * GT:(g + 1) * GT, :]).then_inc(
                    sem(f"xr_in{g % 2}"), 16)

            def load_ffn(i):
                if i >= 2:
                    sp.wait_ge(sem("w_lo_ready"), i - 1)
                sp.dma_start(wraw[i % 2][:, 0:FFN_W[i]], ffn_w[i]).then_inc(sem(f"wraw_in{i % 2}"), 16)

            def store(f):
                sp.wait_ge(sem("fin_ready"), FT * (f + 1))
                sp.dma_start(out.rearrange("(t p) d -> p t d", p=P)[:, f * FT:(f + 1) * FT, :],
                             fin[f % 2][:, :, :]).then_inc(sem(f"out_done{f % 2}"), 16)

            sp.dma_start(wp[:, 0:1, :], proj_w[:, 0:1, :]).then_inc(sem("wq_in"), 16)
            load_x_cols(0)
            sp.dma_start(wp[:, 1:6, :], proj_w[:, 1:6, :]).then_inc(sem("wp_in"), 16)
            sp.dma_start(cst[:, :], consts).then_inc(sem("cst_in"), 16)
            sp.dma_start(gw[:, :], gates_w).then_inc(sem("gw_in"), 16)
            sp.dma_start(sc[:, :], scales).then_inc(sem("sc_in"), 16)
            load_ffn(0)
            load_ffn(1)
            load_x_cols(1)
            load_x_rows(0)
            sp.dma_start(row[:, :], r_out_w).then_inc(sem("row_in"), 16)
            sp.dma_start(wo[:, :], out_w).then_inc(sem("wo_in"), 16)
            load_ffn(2)
            load_ffn(3)
            load_x_rows(1)
            load_x_cols(2)
            load_x_cols(3)
            load_x_rows(2)
            for f in range(FB):
                if f == 2:
                    load_x_rows(3)
                store(f)
            for i in range(2):
                sp.wait_ge(sem(f"out_done{i}"), 16 * FB // 2)

        @block.gpsimd
        def _(pool):
            pool.memset(warm[:, 0:1], 0.0).then_inc(sem("warm_set"), 1)
            for i in range(2):
                pool.memset(vx[i][:, :, :, :, :], 0.0).then_inc(sem("vx_zero"), 1)
            pool.memset(negh[:, :], -0.5).then_inc(sem("negh_set"), 1)

            def front(_, g):
                if g >= 1:
                    pool.wait_ge(sem("scores_done"), GT * g)
                if g % GPB:
                    pool.wait_ge(sem("kc_ready"), NC * g)
                    pool.tensor_copy(kc[:, :, 0:W], kc[:, :, GN:GN + W]).then_inc(sem("k_front"), 1)
                else:
                    pool.memset(kc[:, :, 0:W], 0.0).then_inc(sem("k_front"), 1)

            def rstd(i, n, var, power, rec, signal):
                pool.wait_ge(sem(var), i + 1)
                if i == 0:
                    pool.wait_ge(sem("negh_set"), 1)
                pool.tensor_tensor(rec, power, negh[:, 0:n], ALU.pow).then_inc(sem(signal), 1)

            def split_w(i):
                n = FFN_W[i]
                pool.wait_ge(sem("w_hi_ready"), i + 1)
                pool.tensor_tensor(w_lo[i][:, :], wraw[i % 2][:, 0:n], w_hi[i][:, :].bitcast(F32), ALU.subtract).then_inc(
                    sem("w_lo_ready"), 1)

            def split_h(f, stage, j):
                if f == FB - 1:
                    return
                pool.wait_ge(sem(f"hi{stage}_ready"), 2 * f + j + 1)
                c = slice(2 * j, 2 * j + 2)
                pool.tensor_tensor(h_lo[stage][:, c, :], hf[stage][:, c, :], h_hi[stage][:, c, :].bitcast(F32),
                                   ALU.subtract).then_inc(sem(f"lo{stage}_ready"), 1)

            def first_rstd(t):
                i = t % GT
                rstd(t, 1, "var_ready", ve[:, i:i + 1], rs[:, i:i + 1], "rstd_ready")

            def second_rstd(f):
                rstd(f, FT, "var2_ready", ve2[:, :], rs2[:, :], "rstd2_ready")

            do = {"front": front, "split": split_w, "lo": split_h, "rstd": first_rstd, "rstd2": second_rstd}
            for kind, *at in work_of("Pool"):
                do[kind](*at)

        @block.scalar
        def _(act):
            act.wait_ge(sem("warm_set"), 1)

            def out_of(name, g):
                if name == "qa":
                    wait_full(act, ("q", g))
                    if g == 0:
                        act.wait_ge(sem("q_zero"), 1)
                    else:
                        act.wait_ge(sem("scores_done"), GT * g)
                    for a in range(NA):
                        r = slice(32 * a, 32 * a + 32)
                        act.activation(qa[r, a, :], bank(("q", g))[r, :], ACT.Copy, scale=QK_SCALE).then_inc(sem("qa_ready"), 1)
                elif name == "qt":
                    wait_full(act, ("q", g))
                    if g >= 1:
                        act.wait_ge(sem("zr_mm"), g)
                    act.activation(qt[:, :], bank(("q", g))[:, :], ACT.Copy).then_inc(sem("qt_ready"), 1)
                elif name == "gq":
                    wait_full(act, ("gq", g))
                    if g == 0:
                        act.wait_ge(sem("q_zero"), 2)
                    else:
                        act.wait_ge(sem("lscores_done"), GT * g)
                    for a in range(NA):
                        r = slice(32 * a, 32 * a + 32)
                        act.activation(gqa[r, a, :], bank(("gq", g))[r, :], ACT.Copy, scale=QK_SCALE).then_inc(sem("gqa_ready"), 1)
                else:
                    if g >= 2:
                        act.wait_ge(sem("comb_ready"), GT * (g - 1))
                    wait_full(act, (name, g))
                    act.activation(gate[g % 2][:, ("zl", "zr").index(name), :], bank((name, g))[:, :], ACT.Tanh,
                                   scale=0.5).then_inc(sem("gate_ready"), 1)

            def exp(t):
                act.wait_ge(sem("sub_ready"), t + 1)
                v = pr[t % 2][:, :, :, :]
                act.activation(v, v, ACT.Exp).then_inc(sem("exp_ready"), 1)

            def latent_exp(t):
                act.wait_ge(sem("lsub_ready"), t + 1)
                v = lpr[t % 2][:, :, :, 0:latents(t)]
                act.activation(v, v, ACT.Exp).then_inc(sem("lexp_ready"), 1)

            def upper(f, stage, j):
                act.wait_ge(sem(f"hidden{stage}_ready"), f * M + 2 * j + 2)
                if j == 0 and f >= 1:
                    act.wait_ge(sem(("h1_mm", "h2_mm", "z_mm")[stage]), (2, 2, 1)[stage] * f)
                c = slice(2 * j, 2 * j + 2)
                act.activation(h_hi[stage][:, c, :], hf[stage][:, c, :], ACT.Copy).then_inc(sem(f"hi{stage}_ready"), 1)

            def silu_of(f, j):
                u = f * M + j
                wait_full(act, ("ab", f, j))
                if u == 0:
                    act.wait_ge(sem("sc_in"), 16)
                if u >= 2:
                    act.wait_ge(sem("hidden0_ready"), u - 1)
                act.activation(silu[u % 2][:, :], bank(("ab", f, j))[:, 0:FN], ACT.Silu,
                               scale=sc[:, j:j + 1]).then_inc(sem("silu_ready"), 1)

            def gelu(f, stage, m):
                use = (f"h{stage}", f, m // 2)
                wait_full(act, use)
                if m % 2 == 0 and f >= 1:
                    act.wait_ge(sem(f"lo{stage}_ready"), 2 * (f - 1) + m // 2 + 1)
                act.activation(hf[stage][:, m, :], bank(use)[:, m % 2 * FN:(m % 2 + 1) * FN], ACT.Gelu,
                               scale=s_h[stage - 1][:, m:m + 1]).then_inc(sem(f"hidden{stage}_ready"), 1)

            def down_out(f):
                wait_full(act, ("z", f))
                if f >= 1:
                    act.wait_ge(sem("zt_mm"), f)
                act.activation(zs[:, :], bank(("z", f))[:, 0:FN], ACT.Copy, scale=s_dn).then_inc(sem("zs_ready"), 1)

            def x1_hi_cols(t):
                f, i = t // FT, t % GT
                act.wait_ge(sem("x1t_mm"), t + 1)
                if t % FT == 0 and f >= 2:
                    act.wait_ge(sem("ab_mm"), M * (f - 1))
                act.activation(x1_hi[:, i * P:(i + 1) * P], mix_ps[:, 0:P], ACT.Copy).then_inc(sem("x1_hi_ready"), 1)

            def split_w(i):
                n = FFN_W[i]
                act.wait_ge(sem(f"wraw_in{i % 2}"), 16 * (i // 2 + 1))
                act.activation(w_hi[i][:, :], wraw[i % 2][:, 0:n], ACT.Copy).then_inc(sem("w_hi_ready"), 1)

            act.activation(warm[:, 1:2], warm[:, 0:1], ACT.Exp).then_inc(sem("table_in"), 1)
            do = {"out": out_of, "exp": exp, "lexp": latent_exp, "silu": silu_of, "gelu": gelu, "hi": upper, "zs": down_out,
                  "x1_hi": x1_hi_cols, "split": split_w}
            for kind, *at in work_of("ACT"):
                do[kind](*at)

        @block.vector
        def _(dve):
            def constants_on_chip():
                dve.memset(qa[:, :, :], 0.0).then_inc(sem("q_zero"), 1)
                dve.memset(gqa[:, :, :], 0.0).then_inc(sem("q_zero"), 1)
                for i in range(2):
                    dve.memset(gvx[i][:, :, :, :, :], 0.0).then_inc(sem("l_zero"), 1)
                dve.wait_ge(sem("cst_in"), 16)
                dve.tensor_copy(idb[:, :], ident).then_inc(sem("masks_ready"), 1)
                dve.tensor_copy(maskb[:, :], cst[:, C_WIN:C_LAT + LATW]).then_inc(sem("masks_ready"), 1)
                dve.wait_ge(sem("gw_in"), 16)
                for i in range(2):
                    dve.tensor_scalar(gpat[:, i, :], cst[:, C_PATT:C_PATT + 128], gw[:, i:i + 1], None,
                                      ALU.mult).then_inc(sem("gpat_ready"), 1)

            def pool_x(name, g):
                if name == "x":
                    g += 1
                if g == GROUPS:
                    return
                dve.wait_ge(sem(f"xT_in{g % 2}"), 16 * (g // 2 + 1))
                if g >= 1:
                    dve.wait_ge(sem("gkv_mm"), g)
                dve.tensor_reduce(xpool[:, :], xT[g % 2][:, :].rearrange("p (n c) -> p n c", c=CHUNK),
                                  AX.X, ALU.add).then_inc(sem("xpool_ready"), 1)

            def out_of(name, g):
                b, n0 = g // GPB, (g % GPB) * GL
                if name == "k":
                    wait_full(dve, ("k", g))
                    dve.wait_ge(sem("k_front"), g + 1)
                    for c in range(NC):
                        dve.tensor_scalar(kc[:, c, W:W + GN], bank(("k", g))[:, :], cst[:, C_CM + c:C_CM + c + 1], None,
                                          ALU.mult).then_inc(sem("kc_ready"), 1)
                elif name == "v":
                    wait_full(dve, ("v", g))
                    if g == 0:
                        dve.wait_ge(sem("vx_zero"), 2)
                    elif g >= 2:
                        dve.wait_ge(sem("pv_done"), GT * (g - 1) + 1)
                    for a in range(NA):
                        r = slice(32 * a, 32 * a + 32)
                        dve.transpose(vx[g % 2][r, :, :, a, :],
                                      bank(("v", g))[r, :].rearrange("p (b c d) -> p b c d", c=NC, d=HD)).then_inc(sem("vx_ready"), 1)
                elif name == "gk":
                    wait_full(dve, ("gkv", g))
                    for c in range(LC):
                        dve.tensor_scalar(gkc[b % 2][:, c, n0:n0 + GL], bank(("gkv", g))[:, 0:GL],
                                          cst[:, C_LM + c:C_LM + c + 1], 1.0 / CHUNK, ALU.mult, ALU.mult).then_inc(sem("gkc_ready"), 1)
                else:
                    wait_full(dve, ("gkv", g))
                    if g >= 1:
                        dve.wait_ge(sem("gvr_ready"), g)
                    dve.tensor_scalar(gvt[:, :], bank(("gkv", g))[:, GL:2 * GL], 1.0 / CHUNK, None, ALU.mult).then_inc(sem("gvt_ready"), 1)
                    dve.wait_ge(sem("gvt_ready"), g + 1)
                    if g >= 1:
                        dve.wait_ge(sem("gvx_ready"), NA * g)
                    dve.transpose(gvr[:, :], gvt[:, :]).then_inc(sem("gvr_ready"), 1)
                    dve.wait_ge(sem("gvr_ready"), g + 1)
                    if g == 0:
                        dve.wait_ge(sem("l_zero"), 2)
                    for a in range(NA):
                        r = slice(32 * a, 32 * a + 32)
                        dve.tensor_copy(gvx[b % 2][r, n0 // 32, :, a, :],
                                        gvr[r, 0:LC * HD].rearrange("p (c d) -> p c d", c=LC)).then_inc(sem("gvx_ready"), 1)

            local = scores_ps[:, :, :].rearrange("p k (r j) -> p (k r) j", j=2 * W)

            def row_max(t):
                dve.wait_ge(sem("scores_done"), t + 1)
                if t >= 1:
                    dve.wait_ge(sem("sub_ready"), t)
                dve.tensor_reduce(mx[:, :], local, AX.X, ALU.max).then_inc(sem("max_ready"), 1)

            def shift(t):
                dve.wait_ge(sem("max_ready"), t + 1)
                if t >= 2:
                    dve.wait_ge(sem("prT_ready"), t - 1)
                dve.tensor_tensor(pr[t % 2][:, :, :, :].rearrange("p b c j -> p (b c) j"), local,
                                  mx[:, :].unsqueeze(2).to_broadcast([P, BPT * NC, 2 * W]), ALU.subtract).then_inc(sem("sub_ready"), 1)

            def latent_max(t):
                s = lscores_ps[:, :, :, 0:latents(t)].rearrange("p b c n -> p (b c) n")
                dve.wait_ge(sem("lscores_done"), t + 1)
                if t >= 1:
                    dve.wait_ge(sem("lsub_ready"), t)
                dve.tensor_reduce(lmx[:, :], s, AX.X, ALU.max).then_inc(sem("lmax_ready"), 1)

            def latent_shift(t):
                n = latents(t)
                s = lscores_ps[:, :, :, 0:n].rearrange("p b c n -> p (b c) n")
                dve.wait_ge(sem("lmax_ready"), t + 1)
                if t >= 2:
                    dve.wait_ge(sem("lprT_ready"), LC * (t - 1))
                dve.tensor_tensor(lpr[t % 2][:, :, :, 0:n].rearrange("p b c n -> p (b c) n"), s,
                                  lmx[:, :].unsqueeze(2).to_broadcast([P, BPT * LC, n]), ALU.subtract).then_inc(sem("lsub_ready"), 1)

            def turn(t):
                dve.wait_ge(sem("exp_ready"), t + 1)
                if t >= 1:
                    dve.wait_ge(sem("pv_done"), t)
                dve.transpose(prT[:, :, :, :].rearrange("p c b j -> p b c j"), pr[t % 2][:, :, :, :]).then_inc(sem("prT_ready"), 1)

            def latent_turn(t):
                dve.wait_ge(sem("lexp_ready"), t + 1)
                if t >= 1:
                    dve.wait_ge(sem("lpv_done"), t)
                n = latents(t) // 32
                for c in range(LC):
                    dve.transpose(lprT[:, c, 0:n, :, :].rearrange("p n b q -> p b n q"),
                                  lpr[t % 2][:, :, c, 0:32 * n].rearrange("p b (n j) -> p b n j", j=32)).then_inc(sem("lprT_ready"), 1)

            def latent_reciprocals(t):
                dve.wait_ge(sem("lpv_done"), t + 1)
                if t >= 1:
                    dve.wait_ge(sem("remp_ready"), t)
                dve.reciprocal(rlden[:, :], pv_ps[64:128, 2, :]).then_inc(sem("rlden_ready"), 1)

            def latent_weigh(t):
                dve.wait_ge(sem("rlden_ready"), t + 1)
                if t >= 1:
                    dve.wait_ge(sem("rem_mm"), t)
                dve.tensor_tensor(remp[:, :], pv_ps[0:64, 2, :], rlden[:, :], ALU.mult).then_inc(sem("remp_ready"), 1)

            def reciprocals(t):
                dve.wait_ge(sem("lpv_done"), t + 1)
                if t >= 1:
                    dve.wait_ge(sem("loc_ready"), 2 * t)
                dve.reciprocal(rden[:, :], pv_ps[:, 1, :]).then_inc(sem("rden_ready"), 1)

            def weigh(t):
                dve.wait_ge(sem("rden_ready"), t + 1)
                if t >= 1:
                    dve.wait_ge(sem("comb_ready"), t)
                dve.tensor_tensor(loc[:, :], pv_ps[:, 0, :], rden[:, :], ALU.mult).then_inc(sem("loc_ready"), 1)

            def gated_local(t):
                g, i = t // GT, t % GT
                dve.wait_ge(sem("loc_ready"), 2 * t + 1)
                dve.wait_ge(sem("gate_ready"), 2 * (g + 1))
                cols = slice(i * P, (i + 1) * P)
                dve.scalar_tensor_tensor(out=loc[:, :], in0=gate[g % 2][:, 0, cols], scalar=1.0, in1=loc[:, :],
                                         op0=ALU.add, op1=ALU.mult).then_inc(sem("loc_ready"), 1)

            def gated_remote(t):
                g, i = t // GT, t % GT
                cols = slice(i * P, (i + 1) * P)
                dve.wait_ge(sem("rem_mm"), t + 1)
                dve.wait_ge(sem("gate_ready"), 2 * (g + 1))
                if t >= 1:
                    dve.wait_ge(sem("comb_ready"), t)
                dve.scalar_tensor_tensor(out=rmt[:, :], in0=gate[g % 2][:, 1, cols], scalar=1.0, in1=mix_ps[:, 0:P],
                                         op0=ALU.add, op1=ALU.mult).then_inc(sem("rmt_ready"), 1)

            def combine(t):
                dve.wait_ge(sem("rmt_ready"), t + 1)
                dve.wait_ge(sem("loc_ready"), 2 * t + 2)
                if t >= 1:
                    dve.wait_ge(sem("y_mm"), t)
                dve.tensor_tensor(comb[:, :], loc[:, :], rmt[:, :], ALU.add).then_inc(sem("comb_ready"), 1)

            def first_sum(t):
                g, i = t // GT, t % GT
                dve.wait_ge(sem("y_mm"), t + 1)
                if i == 0:
                    dve.wait_ge(sem(f"xr_in{g % 2}"), 16 * (g // 2 + 1))
                if t >= GT:
                    dve.wait_ge(sem("x1_ready"), t - GT + 1)
                dve.scalar_tensor_tensor(out=res[:, i, :], in0=mix_ps[:, 0:D], scalar=0.5, in1=xr[g % 2][:, i, :],
                                         op0=ALU.mult, op1=ALU.add).then_inc(sem("res_ready"), 1)

            def first_stats(t):
                dve.wait_ge(sem("res_ready"), t + 1)
                dve.bn_stats(st[:, t % GT, :], res[:, t % GT, :]).then_inc(sem("stats_ready"), 1)

            def first_aggr(t):
                dve.wait_ge(sem("stats_ready"), t + 1)
                dve.bn_aggr(mv[:, t % GT, :], st[:, t % GT, :]).then_inc(sem("aggr_ready"), 1)

            def first_eps(t):
                i = t % GT
                dve.wait_ge(sem("aggr_ready"), t + 1)
                dve.tensor_scalar(ve[:, i:i + 1], mv[:, i, 1:2], EPS, None, ALU.add).then_inc(sem("var_ready"), 1)

            def x1_rows(t):
                f, i = t // FT, t % GT
                if f >= 4 and t % FT == 0:
                    dve.wait_ge(sem("res2_ready"), f - 3)
                dve.wait_ge(sem("rstd_ready"), t + 1)
                dve.tensor_scalar(x1[(t // GT) % 2][:, i, :], res[:, i, :], mv[:, i, 0:1], rs[:, i:i + 1],
                                  ALU.subtract, ALU.mult).then_inc(sem("x1_ready"), 1)

            def multiply(f, j):
                wait_full(dve, ("ab", f, j))
                dve.wait_ge(sem("silu_ready"), f * M + j + 1)
                if j % 2 == 0 and f >= 1:
                    dve.wait_ge(sem("lo0_ready"), 2 * (f - 1) + j // 2 + 1)
                dve.scalar_tensor_tensor(out=hf[0][:, j, :], in0=bank(("ab", f, j))[:, FN:2 * FN],
                                         scalar=sc[:, M + j:M + j + 1], in1=silu[j % 2][:, :],
                                         op0=ALU.mult, op1=ALU.mult).then_inc(sem("hidden0_ready"), 1)

            def split_h(f, stage, j):
                if f < FB - 1:
                    return
                dve.wait_ge(sem(f"hi{stage}_ready"), 2 * f + j + 1)
                c = slice(2 * j, 2 * j + 2)
                dve.tensor_tensor(h_lo[stage][:, c, :], hf[stage][:, c, :], h_hi[stage][:, c, :].bitcast(F32),
                                  ALU.subtract).then_inc(sem(f"lo{stage}_ready"), 1)

            def second_sum(f):
                t = FT * f
                wait_full(dve, ("zt", f))
                if f >= 1:
                    dve.wait_ge(sem("fin_ready"), FT * f)
                dve.tensor_tensor(res2[:, :, :], bank(("zt", f))[:, 0:FN].rearrange("p (i d) -> p i d", i=FT),
                                  x1[(t // GT) % 2][:, t % GT:t % GT + FT, :], ALU.add).then_inc(sem("res2_ready"), 1)

            def second_stats(f):
                dve.wait_ge(sem("res2_ready"), f + 1)
                for i in range(FT):
                    dve.bn_stats(st2[:, i, :], res2[:, i, :]).then_inc(sem("stats2_ready"), 1)

            def second_aggr(f):
                for i in range(FT):
                    dve.wait_ge(sem("stats2_ready"), FT * f + i + 1)
                    dve.bn_aggr(mv2[:, i, :], st2[:, i, :]).then_inc(sem("aggr2_ready"), 1)

            def second_eps(f):
                dve.wait_ge(sem("aggr2_ready"), FT * (f + 1))
                dve.tensor_scalar(ve2[:, :], mv2[:, :, 1], EPS, None, ALU.add).then_inc(sem("var2_ready"), 1)

            def final(f):
                dve.wait_ge(sem("rstd2_ready"), f + 1)
                if f >= 2:
                    dve.wait_ge(sem(f"out_done{f % 2}"), 16 * (f // 2))
                for i in range(FT):
                    dve.tensor_scalar(fin[f % 2][:, i, :], res2[:, i, :], mv2[:, i, 0:1], rs2[:, i:i + 1],
                                      ALU.subtract, ALU.mult).then_inc(sem("fin_ready"), 1)

            def x1_lo_cols(t):
                i = t % GT
                dve.wait_ge(sem("x1_hi_ready"), t + 1)
                cols = slice(i * P, (i + 1) * P)
                dve.tensor_tensor(x1_lo[:, cols], mix_ps[:, 0:P], x1_hi[:, cols].bitcast(F32), ALU.subtract).then_inc(
                    sem("x1_lo_ready"), 1)

            def check_w(i):
                dve.wait_ge(sem("w_lo_ready"), i + 1)
                dve.tensor_reduce(w_max[:, i:i + 1], w_lo[i][:, :].bitcast(F32), AX.X, ALU.max,
                                  apply_absolute_value=True).then_inc(sem("w_max_ready"), 1)

            def flag_rows(_):
                n = len(FFN_W)
                dve.wait_ge(sem("w_max_ready"), n)
                dve.tensor_reduce(w_max[:, n:n + 1], w_max[:, 0:n], AX.X, ALU.max).then_inc(sem("w_max_ready"), 1)
                wait_full(dve, ("flag", 0))
                dve.tensor_reduce(flag_max[:, :], bank(("flag", 0))[0:1, 0:P], AX.X, ALU.max).then_inc(sem("flag_max_ready"), 1)
                dve.wait_ge(sem("flag_max_ready"), 1)
                dve.tensor_scalar(flag[:, :], flag_max[:, :], 0.0, None, ALU.is_gt).then_inc(sem("flag_ready"), 1)

            constants_on_chip()
            dve.wait_ge(sem("sc_in"), 16)
            do = {"pool": pool_x, "out": out_of, "max": row_max, "sub": shift, "lmax": latent_max, "lsub": latent_shift,
                  "turn": turn, "lturn": latent_turn, "lrecip": latent_reciprocals, "recip": reciprocals,
                  "lweigh": latent_weigh, "weigh": weigh, "gated": gated_local, "rmt": gated_remote, "comb": combine,
                  "res": first_sum, "stats": first_stats, "aggr": first_aggr, "eps": first_eps, "x1_rows": x1_rows,
                  "x1_lo": x1_lo_cols, "mul": multiply, "res2": second_sum, "stats2": second_stats, "aggr2": second_aggr,
                  "eps2": second_eps, "fin": final, "lo": split_h, "check": check_w, "flag": flag_rows}
            for kind, *at in work_of("DVE"):
                do[kind](*at)

        @block.tensor
        def _(pe):
            def proj(kind, g):
                wait_free(pe, (kind, g))
                o = bank((kind, g))
                if kind == "gkv":
                    pe.wait_ge(sem("xpool_ready"), g + 1)
                    pe.matmul(o[:, 0:GL], wp[:, 4, :], xpool[:, :], start=True, stop=True)
                    mm = pe.matmul(o[:, GL:2 * GL], wp[:, 5, :], xpool[:, :], start=True, stop=True)
                elif kind in ("zl", "zr"):
                    pe.wait_ge(sem("qt_ready"), g + 1)
                    if g == 0:
                        pe.wait_ge(sem("gpat_ready"), 2)
                    mm = pe.matmul(o[:, :], gpat[:, ("zl", "zr").index(kind), :], qt[:, :], start=True, stop=True)
                else:
                    pe.wait_ge(sem(f"xT_in{g % 2}"), 16 * (g // 2 + 1))
                    w = {"q": 0, "k": 1, "v": 2, "gq": 3}[kind]
                    if g == 0 and kind == "k":
                        pe.wait_ge(sem("wp_in"), 16)
                    mm = pe.matmul(o[:, :], wp[:, w, :], xT[g % 2][:, :], start=True, stop=True)
                mm.then_inc(sem(f"{kind}_mm"), 1)

            def scores(t):
                g, i = t // GT, t % GT
                if t == 0:
                    pe.wait_ge(sem("masks_ready"), 2)
                if t >= 1:
                    pe.wait_ge(sem("sub_ready"), t)
                if i == 0:
                    pe.wait_ge(sem("qa_ready"), NA * (g + 1))
                    pe.wait_ge(sem("kc_ready"), NC * (g + 1))
                    pe.wait_ge(sem("k_front"), g + 1)
                first = t % TPB == 0
                for k in range(2):
                    if k == 0 and first:
                        for b in range(2):
                            m = maskb[:, 64 * (1 - b):64 * (1 - b) + 64].unsqueeze(1).to_broadcast([P, NC, 2 * W])
                            pe.matmul(scores_ps[:, 0, 256 * b:256 * b + 256], idb[:, :], m, start=(b == 0), stop=False,
                                      skip_group_check=True)
                    else:
                        m = maskb[:, 0:64].unsqueeze(1).to_broadcast([P, 2 * NC, 2 * W])
                        pe.matmul(scores_ps[:, k, :], idb[:, :], m, start=True, stop=False, skip_group_check=True)
                    for b in range(2):
                        w = (i * BPT + 2 * k + b) * W
                        for a in range(NA):
                            mm = pe.matmul(scores_ps[32 * a:32 * a + 32, k, 256 * b:256 * b + 256], qa[:, a, w:w + W],
                                           kc[:, :, w:w + 2 * W], start=False, stop=True, skip_group_check=True)
                mm.then_inc(sem("scores_done"), 1)

            def latent_scores(t):
                g, i = t // GT, t % GT
                if t >= 1:
                    pe.wait_ge(sem("lsub_ready"), t)
                if i == 0:
                    pe.wait_ge(sem("gqa_ready"), NA * (g + 1))
                    pe.wait_ge(sem("gkc_ready"), LC * (g + 1))
                n = latents(t)
                for b in range(BPT):
                    u = 2 * (S // W - 1) - 2 * ((t % TPB) * BPT + b)
                    m = maskb[:, 128 + u:128 + u + n].unsqueeze(1).to_broadcast([P, LC, n])
                    pe.matmul(lscores_ps[:, b, :, 0:n], idb[:, :], m, start=(b == 0), stop=False, skip_group_check=True)
                for b in range(BPT):
                    w = (i * BPT + b) * W
                    for a in range(NA):
                        mm = pe.matmul(lscores_ps[32 * a:32 * a + 32, b, :, 0:n], gqa[:, a, w:w + W],
                                       gkc[(g // GPB) % 2][:, :, 0:n], start=False, stop=True, skip_group_check=True)
                mm.then_inc(sem("lscores_done"), 1)

            def pv(t):
                g, i = t // GT, t % GT
                pe.wait_ge(sem("prT_ready"), t + 1)
                if i == 0:
                    pe.wait_ge(sem("vx_ready"), NA * (g + 1))
                if t >= 1:
                    pe.wait_ge(sem("remp_ready"), t)
                    pe.wait_ge(sem("loc_ready"), 2 * t)
                flat = prT[:, :, :, :].rearrange("p c b j -> p c (b j)")
                for kb in range(-1, BPT):
                    if kb < 0 and t % TPB == 0:
                        continue
                    lo, hi = max(0, kb * 64 + 32), min(256, kb * 64 + 96)
                    if kb < 0:
                        v = vx[g % 2][:, i * BPT - 1] if i else vx[(g - 1) % 2][:, GN // W - 1]
                        lo, hi = 0, 32
                    else:
                        v = vx[g % 2][:, i * BPT + kb]
                    q0 = 32 * max(kb, 0)
                    for c in range(NC):
                        pe.matmul(pv_ps[32 * c:32 * c + 32, 0, q0:q0 + hi - lo], v[:, c, :, :], flat[:, c, lo:hi],
                                  start=(kb == -1 or (kb == 0 and t % TPB == 0)), stop=True, skip_group_check=True)
                halves = prT[:, :, :, :].rearrange("p c b (h q) -> p c h b q", h=2)
                for h in range(2):
                    for c in range(NC):
                        mm = pe.matmul(pv_ps[32 * c:32 * c + 32, 1, :], ones_a, halves[:, c, h, :, :],
                                       start=False, stop=True, skip_group_check=True)
                mm.then_inc(sem("pv_done"), 1)

            def latent_pv(t):
                g, i = t // GT, t % GT
                pe.wait_ge(sem("lprT_ready"), LC * (t + 1))
                if i == 0:
                    pe.wait_ge(sem("gvx_ready"), NA * (g + 1))
                for n in range(latents(t) // 32):
                    for c in range(LC):
                        r = lprT[:, c, n, :, :].rearrange("p b q -> p (b q)")
                        pe.matmul(pv_ps[32 * c:32 * c + 32, 2, :], gvx[(g // GPB) % 2][:, n, c, :, :], r,
                                  start=False, stop=True, skip_group_check=True)
                        mm = pe.matmul(pv_ps[64 + 32 * c:96 + 32 * c, 2, :], ones_a, r,
                                       start=False, stop=True, skip_group_check=True)
                mm.then_inc(sem("lpv_done"), 1)

            def remote(t):
                if t == 0:
                    pe.wait_ge(sem("row_in"), 16)
                else:
                    pe.wait_ge(sem("x1_lo_ready"), t)
                pe.wait_ge(sem("remp_ready"), t + 1)
                pe.matmul(mix_ps[:, 0:P], row[:, :], remp[:, :], start=True, stop=True).then_inc(sem("rem_mm"), 1)

            def y(t):
                if t == 0:
                    pe.wait_ge(sem("wo_in"), 16)
                pe.wait_ge(sem("rmt_ready"), t + 1)
                pe.wait_ge(sem("comb_ready"), t + 1)
                pe.matmul(mix_ps[:, 0:D], comb[:, :], wo[:, :], start=True, stop=True).then_inc(sem("y_mm"), 1)

            def x1_turn(t):
                pe.wait_ge(sem("res_ready"), t + 1)
                pe.wait_ge(sem("x1_ready"), t + 1)
                pe.transpose(mix_ps[:, 0:P], x1[(t // GT) % 2][:, t % GT, :], ident).then_inc(sem("x1t_mm"), 1)

            def products(o, w, cols, hi, lo, first):
                for k, c in enumerate(cols):
                    if first is not None and k % 2 == 0:
                        pe.wait_ge(sem(f"hi{w - 1}_ready"), first + k // 2 + 1)
                    pe.matmul(o, w_hi[w][:, c], hi[k], start=(k == 0), stop=False)
                for k, c in enumerate(cols):
                    if first is not None and k % 2 == 0:
                        pe.wait_ge(sem(f"lo{w - 1}_ready"), first + k // 2 + 1)
                    if k == len(cols) - 1:
                        with pe.If(general[0] != 0):
                            for i, ci in enumerate(cols):
                                pe.matmul(o, w_lo[w][:, ci], hi[i], start=False, stop=False)
                                pe.matmul(o, w_lo[w][:, ci], lo[i], start=False, stop=False)
                    mm = pe.matmul(o, w_hi[w][:, c], lo[k], start=False, stop=(k == len(cols) - 1))
                return mm

            def ffn(f, stage, m):
                use = ffn_use(f, stage, m)
                if stage == 0:
                    if m == 0:
                        pe.wait_ge(sem("x1_hi_ready"), FT * (f + 1))
                        pe.wait_ge(sem("x1_lo_ready"), FT * (f + 1))
                    wait_free(pe, use)
                    x = slice((f % 2) * FN, (f % 2 + 1) * FN)
                    for i in range(2):
                        c = i * HID + m * P
                        mm = products(bank(use)[:, i * FN:(i + 1) * FN], 0, [slice(c, c + P)], [x1_hi[:, x]], [x1_lo[:, x]], None)
                    mm.then_inc(sem("ab_mm"), 1)
                elif stage < 3 or m == 0:
                    half = m % 2
                    if half == 0:
                        wait_free(pe, use)
                    src, n = stage - 1, HID if stage < 3 else D
                    cols = [slice(k * n + m * P, k * n + (m + 1) * P) for k in range(M)]
                    first = 2 * f if m == 0 else None
                    mm = products(bank(use)[:, half * FN:(half + 1) * FN], stage, cols, [h_hi[src][:, k, :] for k in range(M)],
                                  [h_lo[src][:, k, :] for k in range(M)], first)
                    if half or stage == 3:
                        mm.then_inc(sem(f"{use[0]}_mm"), 1)
                else:
                    pe.wait_ge(sem("zs_ready"), f + 1)
                    wait_free(pe, use)
                    for i in range(FT):
                        mm = pe.transpose(bank(use)[:, i * P:(i + 1) * P], zs[:, i * P:(i + 1) * P], ident)
                    mm.then_inc(sem("zt_mm"), 1)

            general = []

            def flag_load(_):
                pe.wait_ge(sem("w_max_ready"), len(FFN_W) + 1)
                wait_free(pe, ("flag", 0))
                n = len(FFN_W)
                pe.transpose(bank(("flag", 0))[0:1, 0:P], w_max[:, n:n + 1], ident).then_inc(sem("flag_mm"), 1)
                pe.wait_ge(sem("flag_ready"), 1)
                general.append(pe.value_load(flag[0:1, 0:1], min_val=0, max_val=1))

            pe.wait_ge(sem("wq_in"), 16)
            do = {"proj": proj, "scores": scores, "lscores": latent_scores, "pv": pv, "lpv": latent_pv, "rem": remote, "y": y,
                  "x1_turn": x1_turn, "ffn": ffn, "flag": flag_load}
            for kind, *at in work_of("PE"):
                do[kind](*at)


def kernel(**inputs):
    import concourse.bacc as bacc
    from concourse.bass_utils import run_bass_kernel_spmd

    f = {k: np.asarray(v) for k, v in inputs.items()}
    x = f["L0_attn_x"].reshape(TOK, D)

    def pad(w):
        o = np.zeros((D, NA, 32), w.dtype)
        o[:, :, 0:LC * HD] = w.reshape(D, NA, LC * HD)
        return o.reshape(D, 128)

    def rows(w, n):
        return w.reshape(NA, n, HD, -1).transpose(1, 0, 2, 3).reshape(NA * n * HD, -1)

    def chunks(w):
        return w.T.reshape(M, P, -1).transpose(1, 0, 2).reshape(P, -1)

    def col(v):
        return v.reshape(-1, P).T

    a, h = "L0_attn_", "L0_ffn_"
    arrays = {
        "x_rows": x,
        "x_cols": x.T,
        "proj_w": np.stack([f[a + "wq"], f[a + "wk"], f[a + "wv"]] + [pad(f[a + n]) for n in ("wgq", "wgk", "wgv")], 1),
        "gates_w": np.stack([f[a + "gate_local_w"].reshape(P), f[a + "gate_remote_w"].reshape(P)], 1),
        "r_out_w": rows(rows(f[a + "r_out_w"], LC).T, NC).T,
        "out_w": rows(f[a + "w_out"], NC),
        "ffn_w0": np.concatenate([f[h + "w1_w"].T, f[h + "w2_w"].T], 1),
        "ffn_w1": chunks(f[h + "h1_w"]),
        "ffn_w2": chunks(f[h + "h2_w"]),
        "ffn_w3": chunks(f[h + "w3_w"]),
        "scales": np.concatenate([col(f[h + n]) for n in ("w1_s", "w2_s", "h1_s", "h2_s", "w3_s")], 1),
        "consts": constants(),
    }
    nc = bacc.Bacc("TRN2", target_bir_lowering=False, num_devices=1)
    arrays = {k: np.ascontiguousarray(v) for k, v in arrays.items()}
    args = [nc.dram_tensor(k, v.shape, mybir.dt.from_np(v.dtype), kind="ExternalInput").ap() for k, v in arrays.items()]
    args.append(nc.dram_tensor("out", (TOK, D), F32, kind="ExternalOutput").ap())
    seq_block(nc, *args)
    r = run_bass_kernel_spmd(nc, [arrays], core_ids=[0])
    return r.results[0]["out"].reshape(B, S, D)
```

```python
from contextlib import ExitStack

import numpy as np

import concourse.bass as bass
from concourse import mybir

F32 = mybir.dt.float32
BF16 = mybir.dt.bfloat16
F32R = mybir.dt.float32r
I32 = mybir.dt.int32
ALU = mybir.AluOpType
ACT = mybir.ActivationFunctionType
AX = mybir.AxisListType

P = 128
D = 128
W = 32
NA, NC = 4, 4
LC = 2
HD = 8
NL = 64
B, S = 2, 1024
CHUNK = S // NL
TOK = B * S
TILES = TOK // P
BPT = P // W
GT = 4
GROUPS = TILES // GT
GN = GT * P
TPB = S // P
GPB = TPB // GT
GL = GN // CHUNK
HID = 512
M = HID // P
FT = 2
FN = FT * P
FB = TILES // FT
RING = 3
NEG = -1.0e30
FFN_W = (2 * HID, M * HID, M * HID, M * D)
EPS = 1e-5
QK_SCALE = 1.0 / float(np.sqrt(HD))

C_ID, C_WIN, C_WIN0 = 0, 128, 192
C_LAT = 256
LATW = NL + 2 * (S // W - 1)
C_PATT = C_LAT + LATW
C_ONE = C_PATT + 128
C_CM = C_ONE + 32
C_LM = C_CM + NC
C_END = C_LM + LC


def latents(t):
    return GL * ((t // GT) % GPB + 1)


def constants():
    p = np.arange(P)
    a, q = p // 32, p % 32
    c = np.zeros((P, C_END), np.float32)
    c[:, C_ID:C_ID + 128] = np.eye(P)
    j = np.arange(2 * W)
    inside = (j[None] > q[:, None]) & (j[None] <= q[:, None] + W)
    c[:, C_WIN:C_WIN + 64] = np.where(inside, 0.0, NEG)
    c[:, C_WIN0:C_WIN0 + 64] = np.where(inside & (j[None] >= W), 0.0, NEG)
    u = np.arange(LATW) - 2 * (S // W - 1)
    c[:, C_LAT:C_LAT + LATW] = np.where(u[None] <= (q[:, None] // CHUNK), 0.0, NEG)
    cols = np.arange(P)
    same = (a[:, None] == (cols[None] // HD) % NA) & ((q // HD)[:, None] == cols[None] // 32)
    c[:, C_PATT:C_PATT + 128] = same
    c[:, C_ONE:C_ONE + 32] = a[:, None] == (np.arange(32)[None] // HD)
    c[:, C_CM:C_CM + NC] = (q // HD)[:, None] == np.arange(NC)[None]
    c[:, C_LM:C_LM + LC] = (q // HD)[:, None] == np.arange(LC)[None]
    return c


def ring_plan():
    order = []
    for kind, *at in work_of("PE"):
        if kind == "proj":
            order.append(tuple(at))
        elif kind == "flag":
            order.append(("flag", 0))
        elif kind == "ffn":
            f, stage, m = at
            if stage in (0, 3) or m % 2 == 0:
                order.append(ffn_use(f, stage, m))
    return {use: n for n, use in enumerate(order)}


def ffn_use(f, stage, m):
    if stage == 3:
        return ("z", f) if m == 0 else ("zt", f)
    return ("ab", f, m) if stage == 0 else (f"h{stage}", f, m // 2)


FIRST, LAST = 2, TILES
ORDER = {
    "PE": (
        [("proj", "k"), ("proj", "q"), ("proj", "gq"), ("scores", 0), ("proj", "gkv"), ("proj", "zl"),
         ("lscores", 0), ("proj", "v"), ("proj", "zr"), ("scores", 1), ("lscores", 1), ("pv", 0), ("lpv", 0),
         ("rem", 0), ("y", 0), ("scores", 2), ("x1_turn", 0), ("lscores", 2), ("pv", 1), ("lpv", 1), ("rem", 1),
         ("y", 1), ("flag", 0)],
        [("scores", 1), ("ffn", 3, 3, 1), ("x1_turn", -1), ("lscores", 1), ("ffn", 1, 0, 0), ("ffn", 1, 0, 1),
         ("ffn", 1, 0, 2), ("pv", 0), ("ffn", 1, 0, 3), ("lpv", 0), ("ffn", 2, 2, 0), ("ffn", 2, 2, 1),
         ("proj", "q"), ("ffn", 2, 2, 2), ("rem", 0), ("proj", "k"), ("ffn", 2, 2, 3), ("y", 0)],
        [("proj", "gq"), ("proj", "gkv"), ("scores", 1), ("ffn", 1, 1, 0), ("ffn", 1, 1, 1), ("x1_turn", -1),
         ("proj", "zl"), ("proj", "v"), ("pv", 0), ("lpv", 0), ("ffn", 1, 1, 2), ("proj", "zr"), ("ffn", 1, 1, 3),
         ("lscores", 1), ("rem", 0), ("ffn", 2, 3, 0), ("y", 0)],
        [("x1_turn", 15), ("ffn", 5, 3, 1), ("ffn", 7, 0, 0), ("ffn", 7, 0, 1), ("ffn", 7, 0, 2), ("ffn", 7, 0, 3),
         ("ffn", 6, 2, 0), ("ffn", 6, 2, 1), ("ffn", 6, 2, 2), ("ffn", 6, 2, 3), ("ffn", 7, 1, 0), ("ffn", 7, 1, 1),
         ("ffn", 7, 1, 2), ("ffn", 7, 1, 3), ("ffn", 6, 3, 0), ("ffn", 6, 3, 1), ("ffn", 7, 2, 0), ("ffn", 7, 2, 1),
         ("ffn", 7, 2, 2), ("ffn", 7, 2, 3), ("ffn", 7, 3, 0), ("ffn", 7, 3, 1)],
    ),
    "ACT": (
        [("out", "qa"), ("out", "gq"), ("out", "qt"), ("split", 0), ("split", 1), ("split", 2), ("exp", 0),
         ("out", "zl"), ("out", "zr"), ("lexp", 0), ("check", 0), ("exp", 1), ("split", 3), ("check", 1),
         ("check", 2), ("lexp", 1), ("check", 3), ("x1_hi", 0)],
        [("exp", 0), ("x1_hi", -1), ("lexp", 0), ("silu", 1, 0), ("silu", 1, 1), ("silu", 1, 2), ("silu", 1, 3),
         ("hi", 1, 0, 0), ("hi", 1, 0, 1), ("gelu", 2, 2, 0), ("gelu", 2, 2, 1), ("out", "qt"), ("out", "qa"),
         ("hi", 2, 2, 0), ("gelu", 2, 2, 2), ("gelu", 2, 2, 3)],
        [("hi", 2, 2, 1), ("exp", 0), ("out", "gq"), ("lexp", 0), ("x1_hi", -1), ("gelu", 1, 1, 0),
         ("gelu", 1, 1, 1), ("hi", 1, 1, 0), ("out", "zl"), ("gelu", 1, 1, 2), ("gelu", 1, 1, 3), ("out", "zr"),
         ("hi", 1, 1, 1), ("zs", 2)],
        [("x1_hi", 15), ("silu", 7, 0), ("silu", 7, 1), ("silu", 7, 2), ("hi", 7, 0, 0), ("silu", 7, 3),
         ("gelu", 6, 2, 0), ("hi", 7, 0, 1), ("gelu", 6, 2, 1), ("hi", 6, 2, 0), ("gelu", 6, 2, 2),
         ("gelu", 6, 2, 3), ("hi", 6, 2, 1), ("gelu", 7, 1, 0), ("gelu", 7, 1, 1), ("hi", 7, 1, 0),
         ("gelu", 7, 1, 2), ("gelu", 7, 1, 3), ("hi", 7, 1, 1), ("zs", 6), ("gelu", 7, 2, 0), ("gelu", 7, 2, 1),
         ("hi", 7, 2, 0), ("gelu", 7, 2, 2), ("gelu", 7, 2, 3), ("hi", 7, 2, 1), ("zs", 7)],
    ),
    "DVE": (
        [("out", "k"), ("pool", "x0"), ("out", "gk"), ("max", 0), ("out", "gv"), ("sub", 0), ("out", "v"),
         ("lmax", 0), ("pool", "x"), ("lsub", 0), ("turn", 0), ("lturn", 0), ("max", 1), ("lrecip", 0), ("recip", 0),
         ("lweigh", 0), ("weigh", 0), ("sub", 1), ("gated", 0), ("rmt", 0), ("comb", 0), ("res", 0), ("stats", 0),
         ("aggr", 0), ("lmax", 1), ("lsub", 1), ("eps", 0), ("x1_rows", 0), ("max", 2), ("turn", 1), ("sub", 2),
         ("lturn", 1), ("x1_lo", 0), ("lrecip", 1), ("lweigh", 1), ("recip", 1), ("weigh", 1), ("rmt", 1),
         ("gated", 1), ("comb", 1), ("flag", 0)],
        [("lmax", 0), ("res", -1), ("stats", -1), ("aggr", -1), ("eps", -1), ("lsub", 0), ("x1_rows", -1),
         ("turn", 0), ("x1_lo", -1), ("lturn", 0), ("res2", 3), ("stats2", 3), ("aggr2", 3), ("mul", 1, 0),
         ("eps2", 3), ("mul", 1, 1), ("mul", 1, 2), ("max", 1), ("mul", 1, 3), ("lrecip", 0), ("recip", 0),
         ("lweigh", 0), ("weigh", 0), ("sub", 1), ("gated", 0), ("rmt", 0), ("comb", 0), ("out", "k"), ("fin", 3)],
        [("res", -1), ("lmax", 0), ("stats", -1), ("aggr", -1), ("eps", -1), ("out", "gk"), ("lsub", 0),
         ("x1_rows", -1), ("out", "gv"), ("turn", 0), ("lturn", 0), ("max", 1), ("pool", "x"), ("x1_lo", -1),
         ("out", "v"), ("sub", 1), ("lrecip", 0), ("lweigh", 0), ("recip", 0), ("weigh", 0), ("rmt", 0),
         ("gated", 0), ("comb", 0)],
        [("res", 15), ("stats", 15), ("aggr", 15), ("eps", 15), ("x1_rows", 15), ("x1_lo", 15), ("res2", 5),
         ("stats2", 5), ("aggr2", 5), ("mul", 7, 0), ("eps2", 5), ("mul", 7, 1), ("mul", 7, 2), ("mul", 7, 3),
         ("fin", 5), ("lo", 7, 0, 0), ("lo", 7, 0, 1), ("lo", 7, 1, 0), ("lo", 7, 1, 1), ("res2", 6), ("stats2", 6),
         ("aggr2", 6), ("eps2", 6), ("fin", 6), ("lo", 7, 2, 0), ("lo", 7, 2, 1), ("res2", 7), ("stats2", 7),
         ("aggr2", 7), ("eps2", 7), ("fin", 7)],
    ),
    "Pool": (
        [("front", "k"), ("split", 0), ("split", 1), ("split", 2), ("split", 3), ("rstd", 0)],
        [("rstd", -1), ("rstd2", 3), ("lo", 1, 0, 0), ("lo", 1, 0, 1), ("front", "k"), ("lo", 2, 2, 0),
         ("lo", 2, 2, 1)],
        [("rstd", -1), ("lo", 1, 1, 0), ("lo", 1, 1, 1)],
        [("rstd", 15), ("rstd2", 5), ("lo", 6, 2, 0), ("lo", 6, 2, 1), ("rstd2", 6), ("rstd2", 7)],
    ),
}
FFN_KINDS = ("ffn", "silu", "mul", "gelu", "hi", "lo", "zs", "res2", "stats2", "aggr2", "eps2", "rstd2", "fin")
PROJ_KINDS = ("proj", "out", "front", "pool")


def work_of(engine):
    start, even, odd, end = ORDER[engine]
    out = [(kind, *what, 0) if kind in PROJ_KINDS else (kind, *what) for kind, *what in start]
    for t in range(FIRST, LAST):
        for kind, at, *more in (even, odd)[t % 2]:
            if kind in FFN_KINDS:
                f = t // 2 - at
                if 0 <= f < FB:
                    out.append((kind, f, *more))
            elif kind in PROJ_KINDS:
                if t % GT >= GT // 2 and t // GT + 1 < GROUPS:
                    out.append((kind, at, t // GT + 1))
            elif 0 <= t + at < TILES:
                out.append((kind, t + at))
    return out + end


def seq_block(nc, x_rows, x_cols, proj_w, gates_w, r_out_w, out_w, ffn_w0, ffn_w1, ffn_w2, ffn_w3, scales, consts, out):
    ffn_w = (ffn_w0, ffn_w1, ffn_w2, ffn_w3)
    plan = ring_plan()
    use_at = {n: use for use, n in plan.items()}
    with ExitStack() as ctx:
        def sb(name, shape, dt=F32):
            return ctx.enter_context(nc.sbuf_tensor(name, shape, dt))

        def ps(name, shape):
            return ctx.enter_context(nc.psum_tensor(name, shape, F32))

        sems = {}

        def sem(name):
            if name not in sems:
                sems[name] = ctx.enter_context(nc.semaphore(name))
            return sems[name]

        scores_ps = ps("scores_ps", [P, 2, 512])
        lscores_ps = ps("lscores_ps", [P, BPT, LC, NL])
        pv_ps = ps("pv_ps", [P, 4, 128])
        mix_ps = ps("mix_ps", [P, 512])
        ring = [ps(f"ring{i}", [P, 512]) for i in range(RING)]

        cst = sb("cst", [P, C_END])
        xT = [sb(f"xT{i}", [P, GN]) for i in range(2)]
        xr = [sb(f"xr{i}", [P, GT, D]) for i in range(2)]
        wp = sb("wp", [P, 6, 128])
        gw = sb("gw", [P, 2])
        row = sb("row", [LC * 32, 128])
        wo = sb("wo", [P, 128])
        wraw = [sb(f"wraw{i}", [P, n]) for i, n in enumerate(FFN_W[:3])]
        w_hi = [sb(f"w_hi{i}", [P, n], F32R) for i, n in enumerate(FFN_W)]
        w_lo = [sb(f"w_lo{i}", [P, n], F32R) for i, n in enumerate(FFN_W)]
        w_sum = sb("w_sum", [P, len(FFN_W) + 1])
        flag_max = sb("flag_max", [1, 1])
        flag = sb("flag", [1, 1], I32)
        sc = sb("sc", [P, 4 * M + 1])
        idb = sb("idb", [P, 128], BF16)
        maskb = sb("maskb", [P, 128 + LATW], BF16)
        gpat = sb("gpat", [P, 2, 128])
        warm = sb("warm", [P, 2])
        negh = sb("negh", [P, FT])
        qa = sb("qa", [P, GN // W, NA, W])
        gqa = sb("gqa", [P, GN // W, NA, W])
        kc = sb("kc", [P, NC, W + GN])
        vx = [sb(f"vx{i}", [P, GN // W, NC, NA, HD]) for i in range(2)]
        gate = [sb(f"gate{i}", [P, 2, GN]) for i in range(2)]
        qt = sb("qt", [P, GN])
        xpool = sb("xpool", [P, GL])
        gvt = sb("gvt", [P, GL])
        gvr = sb("gvr", [P, 32])
        gkc = [sb(f"gkc{i}", [P, LC, NL]) for i in range(2)]
        gvx = [sb(f"gvx{i}", [P, NL // 32, LC, NA, HD]) for i in range(2)]
        mx = sb("mx", [P, BPT * NC])
        lmx = sb("lmx", [P, BPT * LC])
        pr = [sb(f"pr{i}", [P, BPT, NC, 2 * W]) for i in range(2)]
        lpr = [sb(f"lpr{i}", [P, BPT, LC, NL]) for i in range(2)]
        prT = sb("prT", [P, NC, BPT, 2 * W])
        lprT = sb("lprT", [P, LC, 2, BPT, 32])
        rden = sb("rden", [P, 128])
        rlden = sb("rlden", [64, 128])
        loc = sb("loc", [P, 128])
        remp = sb("remp", [64, 128])
        rmt = sb("rmt", [P, 128])
        comb = sb("comb", [P, 128])
        res = sb("res", [P, GT, D])
        st = sb("st", [P, GT, 6])
        mv = sb("mv", [P, GT, 2])
        ve = sb("ve", [P, GT])
        rs = sb("rs", [P, GT])
        x1 = [sb(f"x1_{i}", [P, GT, D]) for i in range(2)]
        x1_hi = sb("x1_hi", [P, GN], F32R)
        x1_lo = sb("x1_lo", [P, GN], F32R)
        silu = [sb(f"silu{i}", [P, FN]) for i in range(2)]
        hf = [sb(f"hf{i}", [P, M, FN]) for i in range(3)]
        h_hi = [sb(f"h_hi{i}", [P, M, FN], F32R) for i in range(3)]
        h_lo = [sb(f"h_lo{i}", [P, M, FN], F32R) for i in range(3)]
        zs = sb("zs", [P, FN])
        res2 = sb("res2", [P, FT, D])
        st2 = sb("st2", [P, FT, 6])
        mv2 = sb("mv2", [P, FT, 2])
        ve2 = sb("ve2", [P, FT])
        rs2 = sb("rs2", [P, FT])
        fin = [sb(f"fin{i}", [P, FT, D]) for i in range(2)]

        ident = cst[:, C_ID:C_ID + 128]
        ones_a = cst[:, C_ONE:C_ONE + 32]
        s_h = [sc[:, (2 + i) * M:(3 + i) * M] for i in range(2)]
        s_dn = sc[:, 4 * M:4 * M + 1]

        def bank(use):
            return ring[plan[use] % RING]

        def wait_full(eng, use):
            eng.wait_ge(sem(f"{use[0]}_mm"), number(use) + 1)

        def number(use):
            kind, g, *j = use
            return g * {"ab": M, "h1": 2, "h2": 2}[kind] + j[0] if j else g

        def wait_free(pe, use):
            n = plan[use] - RING
            if n < 0:
                return
            kind, g, *j = use_at[n]
            u = number(use_at[n]) + 1
            readers = {
                "q": (("qa_ready", NA * u), ("qt_ready", u)),
                "gq": (("gqa_ready", NA * u),),
                "k": (("kc_ready", NC * u),),
                "gkv": (("gkc_ready", LC * u), ("gvt_ready", u)),
                "v": (("vx_ready", NA * u),),
                "zl": (("gate_ready", 2 * u - 1),),
                "zr": (("gate_ready", 2 * u),),
                "ab": (("hidden0_ready", u),),
                "h1": (("hidden1_ready", 2 * u),),
                "h2": (("hidden2_ready", 2 * u),),
                "flag": (("flag_max_ready", 1),),
                "z": (("zs_ready", u),),
                "zt": (("res2_ready", u),),
            }[kind]
            for name, value in readers:
                pe.wait_ge(sem(name), value)

        block = ctx.enter_context(nc.Block())

        @block.sync
        def _(sp):
            def load_x_cols(g):
                if g >= 2:
                    sp.wait_ge(sem("v_mm"), g - 1)
                    sp.wait_ge(sem("xpool_ready"), g - 1)
                sp.dma_start(xT[g % 2][:, :], x_cols[:, g * GN:(g + 1) * GN]).then_inc(sem(f"xT_in{g % 2}"), 16)

            def load_x_rows(g):
                if g >= 2:
                    sp.wait_ge(sem("res_ready"), GT * (g - 1))
                sp.dma_start(xr[g % 2][:, :, :], x_rows.rearrange("(t p) d -> p t d", p=P)[:, g * GT:(g + 1) * GT, :]).then_inc(
                    sem(f"xr_in{g % 2}"), 16)

            def load_ffn(i):
                if i >= 3:
                    sp.wait_ge(sem("w_sum_ready"), i - 2)
                sp.dma_start(wraw[i % 3][:, 0:FFN_W[i]], ffn_w[i]).then_inc(sem(f"wraw_in{i % 3}"), 16)

            def store(f):
                sp.wait_ge(sem("fin_ready"), FT * (f + 1))
                sp.dma_start(out.rearrange("(t p) d -> p t d", p=P)[:, f * FT:(f + 1) * FT, :],
                             fin[f % 2][:, :, :]).then_inc(sem(f"out_done{f % 2}"), 16)

            sp.dma_start(wp[:, 0:1, :], proj_w[:, 0:1, :]).then_inc(sem("wq_in"), 16)
            load_x_cols(0)
            sp.dma_start(wp[:, 1:6, :], proj_w[:, 1:6, :]).then_inc(sem("wp_in"), 16)
            sp.dma_start(cst[:, :], consts).then_inc(sem("cst_in"), 16)
            sp.dma_start(gw[:, :], gates_w).then_inc(sem("gw_in"), 16)
            sp.dma_start(sc[:, :], scales).then_inc(sem("sc_in"), 16)
            load_ffn(0)
            load_ffn(1)
            load_x_cols(1)
            load_x_rows(0)
            sp.dma_start(row[:, :], r_out_w).then_inc(sem("row_in"), 16)
            sp.dma_start(wo[:, :], out_w).then_inc(sem("wo_in"), 16)
            load_ffn(2)
            load_ffn(3)
            load_x_rows(1)
            load_x_cols(2)
            load_x_cols(3)
            load_x_rows(2)
            for f in range(FB):
                if f == 2:
                    load_x_rows(3)
                store(f)
            for i in range(2):
                sp.wait_ge(sem(f"out_done{i}"), 16 * FB // 2)

        @block.gpsimd
        def _(pool):
            pool.memset(warm[:, 0:1], 0.0).then_inc(sem("warm_set"), 1)
            for i in range(2):
                pool.memset(vx[i][:, :, :, :, :], 0.0).then_inc(sem("vx_zero"), 1)
            pool.memset(negh[:, :], -0.5).then_inc(sem("negh_set"), 1)

            def front(_, g):
                if g >= 1:
                    pool.wait_ge(sem("scores_done"), GT * g)
                if g % GPB:
                    pool.wait_ge(sem("kc_ready"), NC * g)
                    pool.tensor_copy(kc[:, :, 0:W], kc[:, :, GN:GN + W]).then_inc(sem("k_front"), 1)
                else:
                    pool.memset(kc[:, :, 0:W], 0.0).then_inc(sem("k_front"), 1)

            def rstd(i, n, var, power, rec, signal):
                pool.wait_ge(sem(var), i + 1)
                if i == 0:
                    pool.wait_ge(sem("negh_set"), 1)
                pool.tensor_tensor(rec, power, negh[:, 0:n], ALU.pow).then_inc(sem(signal), 1)

            def split_w(i):
                n = FFN_W[i]
                pool.wait_ge(sem("w_hi_ready"), i + 1)
                pool.tensor_tensor(w_lo[i][:, :], wraw[i % 3][:, 0:n], w_hi[i][:, :].bitcast(F32), ALU.subtract).then_inc(
                    sem("w_lo_ready"), 1)

            def split_h(f, stage, j):
                pool.wait_ge(sem(f"hi{stage}_ready"), 2 * f + j + 1)
                c = slice(2 * j, 2 * j + 2)
                pool.tensor_tensor(h_lo[stage][:, c, :], hf[stage][:, c, :], h_hi[stage][:, c, :].bitcast(F32),
                                   ALU.subtract).then_inc(sem(f"lo{stage}_ready"), 1)

            def first_rstd(t):
                i = t % GT
                rstd(t, 1, "var_ready", ve[:, i:i + 1], rs[:, i:i + 1], "rstd_ready")

            def second_rstd(f):
                rstd(f, FT, "var2_ready", ve2[:, :], rs2[:, :], "rstd2_ready")

            do = {"front": front, "split": split_w, "lo": split_h, "rstd": first_rstd, "rstd2": second_rstd}
            for kind, *at in work_of("Pool"):
                do[kind](*at)

        @block.scalar
        def _(act):
            act.wait_ge(sem("warm_set"), 1)

            def out_of(name, g):
                if name == "qa":
                    wait_full(act, ("q", g))
                    if g == 0:
                        act.wait_ge(sem("q_zero"), 1)
                    else:
                        act.wait_ge(sem("scores_done"), GT * g)
                    for a in range(NA):
                        r = slice(32 * a, 32 * a + 32)
                        act.activation(qa[r, :, a, :], bank(("q", g))[r, :].rearrange("p (b q) -> p b q", q=W), ACT.Copy,
                                       scale=QK_SCALE).then_inc(sem("qa_ready"), 1)
                elif name == "qt":
                    wait_full(act, ("q", g))
                    if g >= 1:
                        act.wait_ge(sem("zr_mm"), g)
                    act.activation(qt[:, :], bank(("q", g))[:, :], ACT.Copy).then_inc(sem("qt_ready"), 1)
                elif name == "gq":
                    wait_full(act, ("gq", g))
                    if g == 0:
                        act.wait_ge(sem("q_zero"), 2)
                    else:
                        act.wait_ge(sem("lscores_done"), GT * g)
                    for a in range(NA):
                        r = slice(32 * a, 32 * a + 32)
                        act.activation(gqa[r, :, a, :], bank(("gq", g))[r, :].rearrange("p (b q) -> p b q", q=W), ACT.Copy,
                                       scale=QK_SCALE).then_inc(sem("gqa_ready"), 1)
                else:
                    if g >= 2:
                        act.wait_ge(sem("comb_ready"), GT * (g - 1))
                    wait_full(act, (name, g))
                    act.activation(gate[g % 2][:, ("zl", "zr").index(name), :], bank((name, g))[:, :], ACT.Tanh,
                                   scale=0.5).then_inc(sem("gate_ready"), 1)

            def exp(t):
                act.wait_ge(sem("sub_ready"), t + 1)
                v = pr[t % 2][:, :, :, :]
                act.activation(v, v, ACT.Exp).then_inc(sem("exp_ready"), 1)

            def latent_exp(t):
                act.wait_ge(sem("lsub_ready"), t + 1)
                v = lpr[t % 2][:, :, :, 0:latents(t)]
                act.activation(v, v, ACT.Exp).then_inc(sem("lexp_ready"), 1)

            def upper(f, stage, j):
                act.wait_ge(sem(f"hidden{stage}_ready"), f * M + 2 * j + 2)
                if j == 0 and f >= 1:
                    act.wait_ge(sem(("h1_mm", "h2_mm", "z_mm")[stage]), (2, 2, 1)[stage] * f)
                c = slice(2 * j, 2 * j + 2)
                act.activation(h_hi[stage][:, c, :], hf[stage][:, c, :], ACT.Copy).then_inc(sem(f"hi{stage}_ready"), 1)

            def silu_of(f, j):
                u = f * M + j
                wait_full(act, ("ab", f, j))
                if u == 0:
                    act.wait_ge(sem("sc_in"), 16)
                if u >= 2:
                    act.wait_ge(sem("hidden0_ready"), u - 1)
                act.activation(silu[u % 2][:, :], bank(("ab", f, j))[:, 0:FN], ACT.Silu,
                               scale=sc[:, j:j + 1]).then_inc(sem("silu_ready"), 1)

            def gelu(f, stage, m):
                use = (f"h{stage}", f, m // 2)
                wait_full(act, use)
                if m % 2 == 0 and f >= 1:
                    act.wait_ge(sem(f"lo{stage}_ready"), 2 * (f - 1) + m // 2 + 1)
                act.activation(hf[stage][:, m, :], bank(use)[:, m % 2 * FN:(m % 2 + 1) * FN], ACT.Gelu,
                               scale=s_h[stage - 1][:, m:m + 1]).then_inc(sem(f"hidden{stage}_ready"), 1)

            def down_out(f):
                wait_full(act, ("z", f))
                if f >= 1:
                    act.wait_ge(sem("zt_mm"), f)
                act.activation(zs[:, :], bank(("z", f))[:, 0:FN], ACT.Copy, scale=s_dn).then_inc(sem("zs_ready"), 1)

            def x1_hi_cols(t):
                f, i = t // FT, t % GT
                act.wait_ge(sem("x1t_mm"), t + 1)
                if t % FT == 0 and f >= 2:
                    act.wait_ge(sem("ab_mm"), M * (f - 1))
                act.activation(x1_hi[:, i * P:(i + 1) * P], mix_ps[:, 0:P], ACT.Copy).then_inc(sem("x1_hi_ready"), 1)

            def split_w(i):
                n = FFN_W[i]
                act.wait_ge(sem(f"wraw_in{i % 3}"), 16 * (i // 3 + 1))
                act.activation(w_hi[i][:, :], wraw[i % 3][:, 0:n], ACT.Copy).then_inc(sem("w_hi_ready"), 1)

            def check_w(i):
                n = FFN_W[i]
                act.wait_ge(sem("w_lo_ready"), i + 1)
                act.activation(wraw[i % 3][:, 0:n], w_lo[i][:, :].bitcast(F32), ACT.Abs, accum_out=w_sum[:, i:i + 1]).then_inc(
                    sem("w_sum_ready"), 1)

            act.activation(warm[:, 1:2], warm[:, 0:1], ACT.Exp).then_inc(sem("table_in"), 1)
            do = {"out": out_of, "exp": exp, "lexp": latent_exp, "silu": silu_of, "gelu": gelu, "hi": upper, "zs": down_out,
                  "x1_hi": x1_hi_cols, "split": split_w, "check": check_w}
            for kind, *at in work_of("ACT"):
                do[kind](*at)

        @block.vector
        def _(dve):
            def constants_on_chip():
                dve.memset(qa[:, :, :, :], 0.0).then_inc(sem("q_zero"), 1)
                dve.memset(gqa[:, :, :, :], 0.0).then_inc(sem("q_zero"), 1)
                for i in range(2):
                    dve.memset(gvx[i][:, :, :, :, :], 0.0).then_inc(sem("l_zero"), 1)
                dve.wait_ge(sem("cst_in"), 16)
                dve.tensor_copy(idb[:, :], ident).then_inc(sem("masks_ready"), 1)
                dve.tensor_copy(maskb[:, :], cst[:, C_WIN:C_LAT + LATW]).then_inc(sem("masks_ready"), 1)
                dve.wait_ge(sem("gw_in"), 16)
                for i in range(2):
                    dve.tensor_scalar(gpat[:, i, :], cst[:, C_PATT:C_PATT + 128], gw[:, i:i + 1], None,
                                      ALU.mult).then_inc(sem("gpat_ready"), 1)

            def pool_x(name, g):
                if name == "x":
                    g += 1
                if g == GROUPS:
                    return
                dve.wait_ge(sem(f"xT_in{g % 2}"), 16 * (g // 2 + 1))
                if g >= 1:
                    dve.wait_ge(sem("gkv_mm"), g)
                dve.tensor_reduce(xpool[:, :], xT[g % 2][:, :].rearrange("p (n c) -> p n c", c=CHUNK),
                                  AX.X, ALU.add).then_inc(sem("xpool_ready"), 1)

            def out_of(name, g):
                b, n0 = g // GPB, (g % GPB) * GL
                if name == "k":
                    wait_full(dve, ("k", g))
                    dve.wait_ge(sem("k_front"), g + 1)
                    for c in range(NC):
                        dve.tensor_scalar(kc[:, c, W:W + GN], bank(("k", g))[:, :], cst[:, C_CM + c:C_CM + c + 1], None,
                                          ALU.mult).then_inc(sem("kc_ready"), 1)
                elif name == "v":
                    wait_full(dve, ("v", g))
                    if g == 0:
                        dve.wait_ge(sem("vx_zero"), 2)
                    elif g >= 2:
                        dve.wait_ge(sem("pv_done"), GT * (g - 1) + 1)
                    for a in range(NA):
                        r = slice(32 * a, 32 * a + 32)
                        dve.transpose(vx[g % 2][r, :, :, a, :],
                                      bank(("v", g))[r, :].rearrange("p (b c d) -> p b c d", c=NC, d=HD)).then_inc(sem("vx_ready"), 1)
                elif name == "gk":
                    wait_full(dve, ("gkv", g))
                    for c in range(LC):
                        dve.tensor_scalar(gkc[b % 2][:, c, n0:n0 + GL], bank(("gkv", g))[:, 0:GL],
                                          cst[:, C_LM + c:C_LM + c + 1], 1.0 / CHUNK, ALU.mult, ALU.mult).then_inc(sem("gkc_ready"), 1)
                else:
                    wait_full(dve, ("gkv", g))
                    if g >= 1:
                        dve.wait_ge(sem("gvr_ready"), g)
                    dve.tensor_scalar(gvt[:, :], bank(("gkv", g))[:, GL:2 * GL], 1.0 / CHUNK, None, ALU.mult).then_inc(sem("gvt_ready"), 1)
                    dve.wait_ge(sem("gvt_ready"), g + 1)
                    if g >= 1:
                        dve.wait_ge(sem("gvx_ready"), NA * g)
                    dve.transpose(gvr[:, :], gvt[:, :]).then_inc(sem("gvr_ready"), 1)
                    dve.wait_ge(sem("gvr_ready"), g + 1)
                    if g == 0:
                        dve.wait_ge(sem("l_zero"), 2)
                    for a in range(NA):
                        r = slice(32 * a, 32 * a + 32)
                        dve.tensor_copy(gvx[b % 2][r, n0 // 32, :, a, :],
                                        gvr[r, 0:LC * HD].rearrange("p (c d) -> p c d", c=LC)).then_inc(sem("gvx_ready"), 1)

            local = scores_ps[:, :, :].rearrange("p k (r j) -> p (k r) j", j=2 * W)

            def row_sum(t):
                dve.wait_ge(sem("scores_done"), t + 1)
                if t >= 1:
                    dve.wait_ge(sem("sub_ready"), t)
                dve.tensor_reduce(mx[:, :], local, AX.X, ALU.max).then_inc(sem("max_ready"), 1)

            def shift(t):
                dve.wait_ge(sem("max_ready"), t + 1)
                if t >= 2:
                    dve.wait_ge(sem("prT_ready"), t - 1)
                dve.tensor_tensor(pr[t % 2][:, :, :, :].rearrange("p b c j -> p (b c) j"), local,
                                  mx[:, :].unsqueeze(2).to_broadcast([P, BPT * NC, 2 * W]), ALU.subtract).then_inc(sem("sub_ready"), 1)

            def latent_max(t):
                s = lscores_ps[:, :, :, 0:latents(t)].rearrange("p b c n -> p (b c) n")
                dve.wait_ge(sem("lscores_done"), t + 1)
                if t >= 1:
                    dve.wait_ge(sem("lsub_ready"), t)
                dve.tensor_reduce(lmx[:, :], s, AX.X, ALU.max).then_inc(sem("lmax_ready"), 1)

            def latent_shift(t):
                n = latents(t)
                s = lscores_ps[:, :, :, 0:n].rearrange("p b c n -> p (b c) n")
                dve.wait_ge(sem("lmax_ready"), t + 1)
                if t >= 2:
                    dve.wait_ge(sem("lprT_ready"), LC * (t - 1))
                dve.tensor_tensor(lpr[t % 2][:, :, :, 0:n].rearrange("p b c n -> p (b c) n"), s,
                                  lmx[:, :].unsqueeze(2).to_broadcast([P, BPT * LC, n]), ALU.subtract).then_inc(sem("lsub_ready"), 1)

            def turn(t):
                dve.wait_ge(sem("exp_ready"), t + 1)
                if t >= 1:
                    dve.wait_ge(sem("pv_done"), t)
                dve.transpose(prT[:, :, :, :].rearrange("p c b j -> p b c j"), pr[t % 2][:, :, :, :]).then_inc(sem("prT_ready"), 1)

            def latent_turn(t):
                dve.wait_ge(sem("lexp_ready"), t + 1)
                if t >= 1:
                    dve.wait_ge(sem("lpv_done"), t)
                n = latents(t) // 32
                for c in range(LC):
                    dve.transpose(lprT[:, c, 0:n, :, :].rearrange("p n b q -> p b n q"),
                                  lpr[t % 2][:, :, c, 0:32 * n].rearrange("p b (n j) -> p b n j", j=32)).then_inc(sem("lprT_ready"), 1)

            def latent_reciprocals(t):
                dve.wait_ge(sem("lpv_done"), t + 1)
                if t >= 1:
                    dve.wait_ge(sem("remp_ready"), t)
                dve.reciprocal(rlden[:, :], pv_ps[64:128, 2, :]).then_inc(sem("rlden_ready"), 1)

            def latent_weigh(t):
                dve.wait_ge(sem("rlden_ready"), t + 1)
                if t >= 1:
                    dve.wait_ge(sem("rem_mm"), t)
                dve.tensor_tensor(remp[:, :], pv_ps[0:64, 2, :], rlden[:, :], ALU.mult).then_inc(sem("remp_ready"), 1)

            def reciprocals(t):
                dve.wait_ge(sem("lpv_done"), t + 1)
                if t >= 1:
                    dve.wait_ge(sem("loc_ready"), 2 * t)
                dve.reciprocal(rden[:, :], pv_ps[:, 1, :]).then_inc(sem("rden_ready"), 1)

            def weigh(t):
                dve.wait_ge(sem("rden_ready"), t + 1)
                if t >= 1:
                    dve.wait_ge(sem("comb_ready"), t)
                dve.tensor_tensor(loc[:, :], pv_ps[:, 0, :], rden[:, :], ALU.mult).then_inc(sem("loc_ready"), 1)

            def gated_local(t):
                g, i = t // GT, t % GT
                dve.wait_ge(sem("loc_ready"), 2 * t + 1)
                dve.wait_ge(sem("gate_ready"), 2 * (g + 1))
                cols = slice(i * P, (i + 1) * P)
                dve.scalar_tensor_tensor(out=loc[:, :], in0=gate[g % 2][:, 0, cols], scalar=1.0, in1=loc[:, :],
                                         op0=ALU.add, op1=ALU.mult).then_inc(sem("loc_ready"), 1)

            def gated_remote(t):
                g, i = t // GT, t % GT
                cols = slice(i * P, (i + 1) * P)
                dve.wait_ge(sem("rem_mm"), t + 1)
                dve.wait_ge(sem("gate_ready"), 2 * (g + 1))
                if t >= 1:
                    dve.wait_ge(sem("comb_ready"), t)
                dve.scalar_tensor_tensor(out=rmt[:, :], in0=gate[g % 2][:, 1, cols], scalar=1.0, in1=mix_ps[:, 0:P],
                                         op0=ALU.add, op1=ALU.mult).then_inc(sem("rmt_ready"), 1)

            def combine(t):
                dve.wait_ge(sem("rmt_ready"), t + 1)
                dve.wait_ge(sem("loc_ready"), 2 * t + 2)
                if t >= 1:
                    dve.wait_ge(sem("y_mm"), t)
                dve.tensor_tensor(comb[:, :], loc[:, :], rmt[:, :], ALU.add).then_inc(sem("comb_ready"), 1)

            def first_sum(t):
                g, i = t // GT, t % GT
                dve.wait_ge(sem("y_mm"), t + 1)
                if i == 0:
                    dve.wait_ge(sem(f"xr_in{g % 2}"), 16 * (g // 2 + 1))
                if t >= GT:
                    dve.wait_ge(sem("x1_ready"), t - GT + 1)
                dve.scalar_tensor_tensor(out=res[:, i, :], in0=mix_ps[:, 0:D], scalar=0.5, in1=xr[g % 2][:, i, :],
                                         op0=ALU.mult, op1=ALU.add).then_inc(sem("res_ready"), 1)

            def first_stats(t):
                dve.wait_ge(sem("res_ready"), t + 1)
                dve.bn_stats(st[:, t % GT, :], res[:, t % GT, :]).then_inc(sem("stats_ready"), 1)

            def first_aggr(t):
                dve.wait_ge(sem("stats_ready"), t + 1)
                dve.bn_aggr(mv[:, t % GT, :], st[:, t % GT, :]).then_inc(sem("aggr_ready"), 1)

            def first_eps(t):
                i = t % GT
                dve.wait_ge(sem("aggr_ready"), t + 1)
                dve.tensor_scalar(ve[:, i:i + 1], mv[:, i, 1:2], EPS, None, ALU.add).then_inc(sem("var_ready"), 1)

            def x1_rows(t):
                f, i = t // FT, t % GT
                if f >= 4 and t % FT == 0:
                    dve.wait_ge(sem("res2_ready"), f - 3)
                dve.wait_ge(sem("rstd_ready"), t + 1)
                dve.tensor_scalar(x1[(t // GT) % 2][:, i, :], res[:, i, :], mv[:, i, 0:1], rs[:, i:i + 1],
                                  ALU.subtract, ALU.mult).then_inc(sem("x1_ready"), 1)

            def multiply(f, j):
                wait_full(dve, ("ab", f, j))
                dve.wait_ge(sem("silu_ready"), f * M + j + 1)
                if j % 2 == 0 and f >= 1:
                    dve.wait_ge(sem("lo0_ready"), 2 * (f - 1) + j // 2 + 1)
                dve.scalar_tensor_tensor(out=hf[0][:, j, :], in0=bank(("ab", f, j))[:, FN:2 * FN],
                                         scalar=sc[:, M + j:M + j + 1], in1=silu[j % 2][:, :],
                                         op0=ALU.mult, op1=ALU.mult).then_inc(sem("hidden0_ready"), 1)

            def split_h(f, stage, j):
                dve.wait_ge(sem(f"hi{stage}_ready"), 2 * f + j + 1)
                c = slice(2 * j, 2 * j + 2)
                dve.tensor_tensor(h_lo[stage][:, c, :], hf[stage][:, c, :], h_hi[stage][:, c, :].bitcast(F32),
                                  ALU.subtract).then_inc(sem(f"lo{stage}_ready"), 1)

            def second_sum(f):
                t = FT * f
                wait_full(dve, ("zt", f))
                if f >= 1:
                    dve.wait_ge(sem("fin_ready"), FT * f)
                dve.tensor_tensor(res2[:, :, :], bank(("zt", f))[:, 0:FN].rearrange("p (i d) -> p i d", i=FT),
                                  x1[(t // GT) % 2][:, t % GT:t % GT + FT, :], ALU.add).then_inc(sem("res2_ready"), 1)

            def second_stats(f):
                dve.wait_ge(sem("res2_ready"), f + 1)
                for i in range(FT):
                    dve.bn_stats(st2[:, i, :], res2[:, i, :]).then_inc(sem("stats2_ready"), 1)

            def second_aggr(f):
                for i in range(FT):
                    dve.wait_ge(sem("stats2_ready"), FT * f + i + 1)
                    dve.bn_aggr(mv2[:, i, :], st2[:, i, :]).then_inc(sem("aggr2_ready"), 1)

            def second_eps(f):
                dve.wait_ge(sem("aggr2_ready"), FT * (f + 1))
                dve.tensor_scalar(ve2[:, :], mv2[:, :, 1], EPS, None, ALU.add).then_inc(sem("var2_ready"), 1)

            def final(f):
                dve.wait_ge(sem("rstd2_ready"), f + 1)
                if f >= 2:
                    dve.wait_ge(sem(f"out_done{f % 2}"), 16 * (f // 2))
                for i in range(FT):
                    dve.tensor_scalar(fin[f % 2][:, i, :], res2[:, i, :], mv2[:, i, 0:1], rs2[:, i:i + 1],
                                      ALU.subtract, ALU.mult).then_inc(sem("fin_ready"), 1)

            def x1_lo_cols(t):
                i = t % GT
                dve.wait_ge(sem("x1_hi_ready"), t + 1)
                cols = slice(i * P, (i + 1) * P)
                dve.tensor_tensor(x1_lo[:, cols], mix_ps[:, 0:P], x1_hi[:, cols].bitcast(F32), ALU.subtract).then_inc(
                    sem("x1_lo_ready"), 1)

            def flag_rows(_):
                n = len(FFN_W)
                dve.wait_ge(sem("w_sum_ready"), n)
                dve.tensor_reduce(w_sum[:, n:n + 1], w_sum[:, 0:n], AX.X, ALU.max).then_inc(sem("w_sum_ready"), 1)
                wait_full(dve, ("flag", 0))
                dve.tensor_reduce(flag_max[:, :], bank(("flag", 0))[0:1, 0:P], AX.X, ALU.max).then_inc(sem("flag_max_ready"), 1)
                dve.wait_ge(sem("flag_max_ready"), 1)
                dve.tensor_scalar(flag[:, :], flag_max[:, :], 0.0, None, ALU.is_gt).then_inc(sem("flag_ready"), 1)

            constants_on_chip()
            dve.wait_ge(sem("sc_in"), 16)
            do = {"pool": pool_x, "out": out_of, "max": row_sum, "sub": shift, "lmax": latent_max, "lsub": latent_shift,
                  "turn": turn, "lturn": latent_turn, "lrecip": latent_reciprocals, "recip": reciprocals,
                  "lweigh": latent_weigh, "weigh": weigh, "gated": gated_local, "rmt": gated_remote, "comb": combine,
                  "res": first_sum, "stats": first_stats, "aggr": first_aggr, "eps": first_eps, "x1_rows": x1_rows,
                  "x1_lo": x1_lo_cols, "mul": multiply, "res2": second_sum, "stats2": second_stats, "aggr2": second_aggr,
                  "eps2": second_eps, "fin": final, "lo": split_h, "flag": flag_rows}
            for kind, *at in work_of("DVE"):
                do[kind](*at)

        @block.tensor
        def _(pe):
            def proj(kind, g):
                wait_free(pe, (kind, g))
                o = bank((kind, g))
                if kind == "gkv":
                    pe.wait_ge(sem("xpool_ready"), g + 1)
                    pe.matmul(o[:, 0:GL], wp[:, 4, :], xpool[:, :], start=True, stop=True)
                    mm = pe.matmul(o[:, GL:2 * GL], wp[:, 5, :], xpool[:, :], start=True, stop=True)
                elif kind in ("zl", "zr"):
                    pe.wait_ge(sem("qt_ready"), g + 1)
                    if g == 0:
                        pe.wait_ge(sem("gpat_ready"), 2)
                    mm = pe.matmul(o[:, :], gpat[:, ("zl", "zr").index(kind), :], qt[:, :], start=True, stop=True)
                else:
                    pe.wait_ge(sem(f"xT_in{g % 2}"), 16 * (g // 2 + 1))
                    w = {"q": 0, "k": 1, "v": 2, "gq": 3}[kind]
                    if g == 0 and kind == "k":
                        pe.wait_ge(sem("wp_in"), 16)
                    mm = pe.matmul(o[:, :], wp[:, w, :], xT[g % 2][:, :], start=True, stop=True)
                mm.then_inc(sem(f"{kind}_mm"), 1)

            def scores(t):
                g, i = t // GT, t % GT
                if t == 0:
                    pe.wait_ge(sem("masks_ready"), 2)
                if t >= 1:
                    pe.wait_ge(sem("sub_ready"), t)
                if i == 0:
                    pe.wait_ge(sem("qa_ready"), NA * (g + 1))
                    pe.wait_ge(sem("kc_ready"), NC * (g + 1))
                    pe.wait_ge(sem("k_front"), g + 1)
                first = t % TPB == 0
                for k in range(2):
                    if k == 0 and first:
                        for b in range(2):
                            m = maskb[:, 64 * (1 - b):64 * (1 - b) + 64].unsqueeze(1).to_broadcast([P, NC, 2 * W])
                            pe.matmul(scores_ps[:, 0, 256 * b:256 * b + 256], idb[:, :], m, start=(b == 0), stop=False,
                                      skip_group_check=True)
                    else:
                        m = maskb[:, 0:64].unsqueeze(1).to_broadcast([P, 2 * NC, 2 * W])
                        pe.matmul(scores_ps[:, k, :], idb[:, :], m, start=True, stop=False, skip_group_check=True)
                    for b in range(2):
                        w = (i * BPT + 2 * k + b) * W
                        mm = pe.matmul(scores_ps[:, k, 256 * b:256 * b + 256], qa[:, w // W, :, :].rearrange("p a q -> p (a q)"), kc[:, :, w:w + 2 * W],
                                       start=False, stop=True, skip_group_check=True)
                mm.then_inc(sem("scores_done"), 1)

            def latent_scores(t):
                g, i = t // GT, t % GT
                if t >= 1:
                    pe.wait_ge(sem("lsub_ready"), t)
                if i == 0:
                    pe.wait_ge(sem("gqa_ready"), NA * (g + 1))
                    pe.wait_ge(sem("gkc_ready"), LC * (g + 1))
                n = latents(t)
                for b in range(BPT):
                    u = 2 * (S // W - 1) - 2 * ((t % TPB) * BPT + b)
                    m = maskb[:, 128 + u:128 + u + n].unsqueeze(1).to_broadcast([P, LC, n])
                    pe.matmul(lscores_ps[:, b, :, 0:n], idb[:, :], m, start=(b == 0), stop=False, skip_group_check=True)
                for b in range(BPT):
                    w = (i * BPT + b) * W
                    mm = pe.matmul(lscores_ps[:, b, :, 0:n], gqa[:, w // W, :, :].rearrange("p a q -> p (a q)"), gkc[(g // GPB) % 2][:, :, 0:n],
                                   start=False, stop=True, skip_group_check=True)
                mm.then_inc(sem("lscores_done"), 1)

            def pv(t):
                g, i = t // GT, t % GT
                pe.wait_ge(sem("prT_ready"), t + 1)
                if i == 0:
                    pe.wait_ge(sem("vx_ready"), NA * (g + 1))
                if t >= 1:
                    pe.wait_ge(sem("remp_ready"), t)
                    pe.wait_ge(sem("loc_ready"), 2 * t)
                flat = prT[:, :, :, :].rearrange("p c b j -> p c (b j)")
                for kb in range(-1, BPT):
                    if kb < 0 and t % TPB == 0:
                        continue
                    lo, hi = max(0, kb * 64 + 32), min(256, kb * 64 + 96)
                    if kb < 0:
                        v = vx[g % 2][:, i * BPT - 1] if i else vx[(g - 1) % 2][:, GN // W - 1]
                        lo, hi = 0, 32
                    else:
                        v = vx[g % 2][:, i * BPT + kb]
                    q0 = 32 * max(kb, 0)
                    for c in range(NC):
                        pe.matmul(pv_ps[32 * c:32 * c + 32, 0, q0:q0 + hi - lo], v[:, c, :, :], flat[:, c, lo:hi],
                                  start=(kb == -1 or (kb == 0 and t % TPB == 0)), stop=True, skip_group_check=True)
                halves = prT[:, :, :, :].rearrange("p c b (h q) -> p c h b q", h=2)
                for h in range(2):
                    for c in range(NC):
                        mm = pe.matmul(pv_ps[32 * c:32 * c + 32, 1, :], ones_a, halves[:, c, h, :, :],
                                       start=False, stop=True, skip_group_check=True)
                mm.then_inc(sem("pv_done"), 1)

            def latent_pv(t):
                g, i = t // GT, t % GT
                pe.wait_ge(sem("lprT_ready"), LC * (t + 1))
                if i == 0:
                    pe.wait_ge(sem("gvx_ready"), NA * (g + 1))
                for n in range(latents(t) // 32):
                    for c in range(LC):
                        r = lprT[:, c, n, :, :].rearrange("p b q -> p (b q)")
                        pe.matmul(pv_ps[32 * c:32 * c + 32, 2, :], gvx[(g // GPB) % 2][:, n, c, :, :], r,
                                  start=False, stop=True, skip_group_check=True)
                        mm = pe.matmul(pv_ps[64 + 32 * c:96 + 32 * c, 2, :], ones_a, r,
                                       start=False, stop=True, skip_group_check=True)
                mm.then_inc(sem("lpv_done"), 1)

            def remote(t):
                if t == 0:
                    pe.wait_ge(sem("row_in"), 16)
                else:
                    pe.wait_ge(sem("x1_lo_ready"), t)
                pe.wait_ge(sem("remp_ready"), t + 1)
                pe.matmul(mix_ps[:, 0:P], row[:, :], remp[:, :], start=True, stop=True).then_inc(sem("rem_mm"), 1)

            def y(t):
                if t == 0:
                    pe.wait_ge(sem("wo_in"), 16)
                pe.wait_ge(sem("rmt_ready"), t + 1)
                pe.wait_ge(sem("comb_ready"), t + 1)
                pe.matmul(mix_ps[:, 0:D], comb[:, :], wo[:, :], start=True, stop=True).then_inc(sem("y_mm"), 1)

            def x1_turn(t):
                pe.wait_ge(sem("res_ready"), t + 1)
                pe.wait_ge(sem("x1_ready"), t + 1)
                pe.transpose(mix_ps[:, 0:P], x1[(t // GT) % 2][:, t % GT, :], ident).then_inc(sem("x1t_mm"), 1)

            def products(o, w, cols, hi, lo, opens, first):
                for k, c in enumerate(cols):
                    if first is not None and k % 2 == 0:
                        pe.wait_ge(sem(f"hi{w - 1}_ready"), first + k // 2 + 1)
                    pe.matmul(o, w_hi[w][:, c], hi[k], start=(opens and k == 0), stop=False, skip_group_check=True)
                for k, c in enumerate(cols[:-1]):
                    if first is not None and k % 2 == 0:
                        pe.wait_ge(sem(f"lo{w - 1}_ready"), first + k // 2 + 1)
                    pe.matmul(o, w_hi[w][:, c], lo[k], start=False, stop=False, skip_group_check=True)

            def close(outs, w, hi, lo):
                with pe.If(general[0] != 0):
                    for o, cols in outs:
                        for k, c in enumerate(cols):
                            pe.matmul(o, w_lo[w][:, c], hi[k], start=False, stop=False, skip_group_check=True)
                            pe.matmul(o, w_lo[w][:, c], lo[k], start=False, stop=False, skip_group_check=True)
                for o, cols in outs:
                    mm = pe.matmul(o, w_hi[w][:, cols[-1]], lo[-1], start=False, stop=True, skip_group_check=True)
                return mm

            def ffn(f, stage, m):
                use = ffn_use(f, stage, m)

                def half(i):
                    return bank(use)[:, i * FN:(i + 1) * FN]

                if stage == 0:
                    if m == 0:
                        pe.wait_ge(sem("x1_hi_ready"), FT * (f + 1))
                        pe.wait_ge(sem("x1_lo_ready"), FT * (f + 1))
                    wait_free(pe, use)
                    x = slice((f % 2) * FN, (f % 2 + 1) * FN)
                    outs = [(half(i), [slice(i * HID + m * P, i * HID + (m + 1) * P)]) for i in range(2)]
                    for i, (o, cols) in enumerate(outs):
                        products(o, 0, cols, [x1_hi[:, x]], [x1_lo[:, x]], i == 0, None)
                    close(outs, 0, [x1_hi[:, x]], [x1_lo[:, x]]).then_inc(sem("ab_mm"), 1)
                elif stage < 3 or m == 0:
                    if m % 2 == 0:
                        wait_free(pe, use)
                    hi, lo = ([x[stage - 1][:, k, :] for k in range(M)] for x in (h_hi, h_lo))
                    n = HID if stage < 3 else D

                    def cols(m):
                        return [slice(k * n + m * P, k * n + (m + 1) * P) for k in range(M)]

                    products(half(m % 2), stage, cols(m), hi, lo, m % 2 == 0, 2 * f if m == 0 else None)
                    if stage == 3:
                        close([(half(0), cols(0))], stage, hi, lo).then_inc(sem("z_mm"), 1)
                    elif m % 2:
                        close([(half(0), cols(m - 1)), (half(1), cols(m))], stage, hi, lo).then_inc(sem(f"{use[0]}_mm"), 1)
                else:
                    pe.wait_ge(sem("zs_ready"), f + 1)
                    wait_free(pe, use)
                    for i in range(FT):
                        mm = pe.transpose(bank(use)[:, i * P:(i + 1) * P], zs[:, i * P:(i + 1) * P], ident)
                    mm.then_inc(sem("zt_mm"), 1)

            general = []

            def flag_load(_):
                pe.wait_ge(sem("w_sum_ready"), len(FFN_W) + 1)
                wait_free(pe, ("flag", 0))
                n = len(FFN_W)
                pe.transpose(bank(("flag", 0))[0:1, 0:P], w_sum[:, n:n + 1], ident).then_inc(sem("flag_mm"), 1)
                pe.wait_ge(sem("flag_ready"), 1)
                general.append(pe.value_load(flag[0:1, 0:1], min_val=0, max_val=1))

            pe.wait_ge(sem("wq_in"), 16)
            do = {"proj": proj, "scores": scores, "lscores": latent_scores, "pv": pv, "lpv": latent_pv, "rem": remote, "y": y,
                  "x1_turn": x1_turn, "ffn": ffn, "flag": flag_load}
            for kind, *at in work_of("PE"):
                do[kind](*at)


def kernel(**inputs):
    import concourse.bacc as bacc
    from concourse.bass_utils import run_bass_kernel_spmd

    f = {k: np.asarray(v) for k, v in inputs.items()}
    x = f["L0_attn_x"].reshape(TOK, D)

    def pad(w):
        o = np.zeros((D, NA, 32), w.dtype)
        o[:, :, 0:LC * HD] = w.reshape(D, NA, LC * HD)
        return o.reshape(D, 128)

    def rows(w, n):
        return w.reshape(NA, n, HD, -1).transpose(1, 0, 2, 3).reshape(NA * n * HD, -1)

    def chunks(w):
        return w.T.reshape(M, P, -1).transpose(1, 0, 2).reshape(P, -1)

    def col(v):
        return v.reshape(-1, P).T

    a, h = "L0_attn_", "L0_ffn_"
    arrays = {
        "x_rows": x,
        "x_cols": x.T,
        "proj_w": np.stack([f[a + "wq"], f[a + "wk"], f[a + "wv"]] + [pad(f[a + n]) for n in ("wgq", "wgk", "wgv")], 1),
        "gates_w": np.stack([f[a + "gate_local_w"].reshape(P), f[a + "gate_remote_w"].reshape(P)], 1),
        "r_out_w": rows(rows(f[a + "r_out_w"], LC).T, NC).T,
        "out_w": rows(f[a + "w_out"], NC),
        "ffn_w0": np.concatenate([f[h + "w1_w"].T, f[h + "w2_w"].T], 1),
        "ffn_w1": chunks(f[h + "h1_w"]),
        "ffn_w2": chunks(f[h + "h2_w"]),
        "ffn_w3": chunks(f[h + "w3_w"]),
        "scales": np.concatenate([col(f[h + n]) for n in ("w1_s", "w2_s", "h1_s", "h2_s", "w3_s")], 1),
        "consts": constants(),
    }
    nc = bacc.Bacc("TRN2", target_bir_lowering=False, num_devices=1)
    arrays = {k: np.ascontiguousarray(v) for k, v in arrays.items()}
    args = [nc.dram_tensor(k, v.shape, mybir.dt.from_np(v.dtype), kind="ExternalInput").ap() for k, v in arrays.items()]
    args.append(nc.dram_tensor("out", (TOK, D), F32, kind="ExternalOutput").ap())
    seq_block(nc, *args)
    r = run_bass_kernel_spmd(nc, [arrays], core_ids=[0])
    return r.results[0]["out"].reshape(B, S, D)
```
